# Optimizing a Trainium2 kernel written in Bass

```python
import numpy as np
import jax
import jax.numpy as jnp

def _softmax(x, axis=-1):
    return jax.nn.softmax(x, axis=axis)

def _gelu(x):
    return jax.nn.gelu(x, approximate=True)

def _silu(x):
    return jax.nn.silu(x)

def _sigmoid(x):
    return jax.nn.sigmoid(x)

def _layernorm(x, axis=-1, eps=1e-05):
    m = jnp.mean(x, axis=axis, keepdims=True)
    v = jnp.var(x, axis=axis, keepdims=True)
    return (x - m) / jnp.sqrt(v + eps)

def _scatter_add(tgt, idx, src, axis=0):
    return tgt.at[idx].add(src)

def _segment_sum(src, seg, n):
    return jax.ops.segment_sum(src, seg, n)
kernel_name = 'mk_macaron_d2_jaxref_r8_5c5668'

def setup_inputs(seed: int=0):
    np.random.seed(seed)
    _w = jnp.asarray

    def _L0_attn_setup():
        import jax, jax.numpy as jnp
        import numpy as np
        D_MODEL = 128
        N_HEADS = 16
        D_K = 64
        key = jax.random.key(seed)
        k0, k1, k2, k3, k4 = jax.random.split(key, 5)
        B, S = (4, 512)
        std = 0.02
        x = jax.random.normal(k0, (B, S, D_MODEL), dtype=jnp.float32)
        W_q = std * jax.random.normal(k1, (N_HEADS * D_K, D_MODEL), dtype=jnp.float32)
        W_k = std * jax.random.normal(k2, (N_HEADS * D_K, D_MODEL), dtype=jnp.float32)
        W_v = std * jax.random.normal(k3, (N_HEADS * D_K, D_MODEL), dtype=jnp.float32)
        W_o = std * jax.random.normal(k4, (D_MODEL, N_HEADS * D_K), dtype=jnp.float32)
        return {'x': x, 'W_q': W_q, 'W_k': W_k, 'W_v': W_v, 'W_o': W_o}
    _L0_attn_in = _L0_attn_setup()

    def _L0_ffn_setup():
        import jax, jax.numpy as jnp
        import numpy as np
        B, S, D, H, E = (4, 256, 128, 512, 8)
        THRESHOLD = 0.5
        key = jax.random.key(seed)
        ks = jax.random.split(key, 7)
        s_in = 1.0 / np.sqrt(D)
        s_h = 1.0 / np.sqrt(H)
        return {'x': jax.random.normal(ks[0], (B, S, D), dtype=jnp.float32), 'Wg': jax.random.uniform(ks[1], (D, E), jnp.float32, -s_in, s_in), 'bg': jax.random.uniform(ks[2], (E,), jnp.float32, -s_in, s_in), 'W1': jax.random.uniform(ks[3], (E, D, H), jnp.float32, -s_in, s_in), 'b1': jax.random.uniform(ks[4], (E, H), jnp.float32, -s_in, s_in), 'W2': jax.random.uniform(ks[5], (E, H, D), jnp.float32, -s_h, s_h), 'b2': jax.random.uniform(ks[6], (E, D), jnp.float32, -s_h, s_h)}
    _L0_ffn_in = _L0_ffn_setup()

    def _L1_attn_setup():
        import jax, jax.numpy as jnp
        import numpy as np
        import math
        DIM = 128
        HEADS = 16
        HEAD_DIM = DIM // HEADS
        SCALE = math.sqrt(HEAD_DIM)

        def _heads(y, B, T):
            return y.reshape(B, T, HEADS, HEAD_DIM).transpose(0, 2, 1, 3)
        key = jax.random.key(seed)
        ks = jax.random.split(key, 7)
        B, T, C = (2, 256, DIM)
        w = 0.02
        return {'x': jax.random.normal(ks[0], (B, T, C), dtype=jnp.float32), 'W_Q': jax.random.normal(ks[1], (C, C), dtype=jnp.float32) * w, 'W_K': jax.random.normal(ks[2], (C, C), dtype=jnp.float32) * w, 'W_V': jax.random.normal(ks[3], (C, C), dtype=jnp.float32) * w, 'W_K_prime': jax.random.normal(ks[4], (C, C), dtype=jnp.float32) * w, 'W_O': jax.random.normal(ks[5], (C, C), dtype=jnp.float32) * w, 'alpha': jnp.float32(0.5)}
    _L1_attn_in = _L1_attn_setup()

    def _L1_ffn_setup():
        import jax, jax.numpy as jnp
        import numpy as np
        DIM = 128
        DEPTH = 6
        HEADS = 16
        DIM_HEAD = 64
        WINDOW = 32
        INNER = HEADS * DIM_HEAD
        DIM_INNER = int(DIM * 4 * 2 / 3)
        QK_SCALE = 8.0

        def shift_tokens(t):
            a, s = jnp.split(t, 2, -1)
            s = jnp.pad(s, ((0, 0), (1, 0), (0, 0)))[:, :-1]
            return jnp.concatenate([a, s], -1)

        def l2norm(t):
            return t / jnp.maximum(jnp.linalg.norm(t, axis=-1, keepdims=True), 1e-12)

        def rotate_half(x):
            x1, x2 = jnp.split(x, 2, -1)
            return jnp.concatenate([-x2, x1], -1)

        def rotary_tables(n):
            half = jnp.arange(0, DIM_HEAD, 2, dtype=jnp.float32)
            inv_freq = 1.0 / 10000.0 ** (half / DIM_HEAD)
            t = jnp.arange(n, dtype=jnp.float32)
            freqs = t[:, None] * inv_freq[None, :]
            freqs = jnp.concatenate([freqs, freqs], -1)
            base_scale = (half + 0.4 * DIM_HEAD) / (1.4 * DIM_HEAD)
            power = (t - n // 2) / (WINDOW // 2)
            scale = base_scale[None, :] ** power[:, None]
            scale = jnp.concatenate([scale, scale], -1)
            return (freqs, scale)

        def local_attention(q, k, v):
            b, h, n, d = q.shape
            w = WINDOW
            nw = n // w
            bq = q.reshape(b, h, nw, w, d)
            bk = k.reshape(b, h, nw, w, d)
            bv = v.reshape(b, h, nw, w, d)

            def look(t):
                p = jnp.pad(t, ((0, 0), (0, 0), (1, 0), (0, 0), (0, 0)))
                return jnp.concatenate([p[:, :, :nw], p[:, :, 1:]], axis=3)
            bk2, bv2 = (look(bk), look(bv))
            seq = jnp.arange(n).reshape(nw, w)
            seq_p = jnp.pad(seq, ((1, 0), (0, 0)), constant_values=-1)
            jt = jnp.concatenate([seq_p[:nw], seq_p[1:]], axis=1)
            it = seq[:, :, None]
            jb = jt[:, None, :]
            mask = (it < jb) | (it > jb + w) | (jb == -1)
            sim = jnp.einsum('bhwie,bhwje->bhwij', bq, bk2) * QK_SCALE
            sim = jnp.where(mask, -jnp.finfo(sim.dtype).max, sim)
            attn = jax.nn.softmax(sim, -1)
            out = jnp.einsum('bhwij,bhwje->bhwie', attn, bv2)
            return out.reshape(b, h, n, d)

        def attn_layer(x, Wqkv, qs, ksc, Wo):
            b, n, _ = x.shape
            qkv = x @ Wqkv
            q, k, v = jnp.split(qkv, 3, -1)
            sh = lambda t: t.reshape(b, n, HEADS, DIM_HEAD).transpose(0, 2, 1, 3)
            q, k, v = (sh(q), sh(k), sh(v))
            q = l2norm(q) * qs
            k = l2norm(k) * ksc
            freqs, scale = rotary_tables(n)
            cos, sin = (jnp.cos(freqs), jnp.sin(freqs))
            q = q * cos * scale + rotate_half(q) * sin * scale
            inv = 1.0 / scale
            k = k * cos * inv + rotate_half(k) * sin * inv
            out = local_attention(q, k, v)
            out = out.transpose(0, 2, 1, 3).reshape(b, n, INNER)
            return out @ Wo

        def ffn_layer(x, g, bln, W1, b1, W2, b2):
            mu = x.mean(-1, keepdims=True)
            var = ((x - mu) ** 2).mean(-1, keepdims=True)
            xn = (x - mu) / jnp.sqrt(var + 1e-05) * g + bln
            hg = xn @ W1 + b1
            a, gate = jnp.split(hg, 2, -1)
            return a * jax.nn.gelu(gate, approximate=False) @ W2 + b2
        key = jax.random.key(seed)
        ks = jax.random.split(key, 8)
        B, N = (2, 256)
        init = lambda k, shape: jax.random.normal(k, shape, jnp.float32) * 0.02
        return {'x': jax.random.normal(ks[0], (B, N, DIM), jnp.float32), 'Wqkv': init(ks[1], (DEPTH, DIM, 3 * INNER)), 'q_scale': jnp.ones((DEPTH, DIM_HEAD), jnp.float32), 'k_scale': jnp.ones((DEPTH, DIM_HEAD), jnp.float32), 'Wo': init(ks[2], (DEPTH, INNER, DIM)), 'ln_g': jnp.ones((DEPTH, DIM), jnp.float32), 'ln_b': jnp.zeros((DEPTH, DIM), jnp.float32), 'W1': init(ks[3], (DEPTH, DIM, 2 * DIM_INNER)), 'b1': jnp.zeros((DEPTH, 2 * DIM_INNER), jnp.float32), 'W2': init(ks[4], (DEPTH, DIM_INNER, DIM)), 'b2': jnp.zeros((DEPTH, DIM), jnp.float32)}
    _L1_ffn_in = _L1_ffn_setup()
    _d = {'L0_attn_x': _L0_attn_in['x'], 'L0_attn_W_q': _L0_attn_in['W_q'], 'L0_attn_W_k': _L0_attn_in['W_k'], 'L0_attn_W_v': _L0_attn_in['W_v'], 'L0_attn_W_o': _L0_attn_in['W_o'], 'L0_ffn_Wg': _L0_ffn_in['Wg'], 'L0_ffn_bg': _L0_ffn_in['bg'], 'L0_ffn_W1': _L0_ffn_in['W1'], 'L0_ffn_b1': _L0_ffn_in['b1'], 'L0_ffn_W2': _L0_ffn_in['W2'], 'L0_ffn_b2': _L0_ffn_in['b2'], 'L1_attn_W_Q': _L1_attn_in['W_Q'], 'L1_attn_W_K': _L1_attn_in['W_K'], 'L1_attn_W_V': _L1_attn_in['W_V'], 'L1_attn_W_K_prime': _L1_attn_in['W_K_prime'], 'L1_attn_W_O': _L1_attn_in['W_O'], 'L1_attn_alpha': _L1_attn_in['alpha'], 'L1_ffn_Wqkv': _L1_ffn_in['Wqkv'], 'L1_ffn_q_scale': _L1_ffn_in['q_scale'], 'L1_ffn_k_scale': _L1_ffn_in['k_scale'], 'L1_ffn_Wo': _L1_ffn_in['Wo'], 'L1_ffn_ln_g': _L1_ffn_in['ln_g'], 'L1_ffn_ln_b': _L1_ffn_in['ln_b'], 'L1_ffn_W1': _L1_ffn_in['W1'], 'L1_ffn_b1': _L1_ffn_in['b1'], 'L1_ffn_W2': _L1_ffn_in['W2'], 'L1_ffn_b2': _L1_ffn_in['b2']}
    _x0 = _d['L0_attn_x']
    _d['L0_attn_x'] = jax.random.normal(jax.random.fold_in(jax.random.key(seed), 1), (4, 512, 128), dtype=_x0.dtype)
    del _x0
    return _d

def reference(L0_attn_x, L0_attn_W_q, L0_attn_W_k, L0_attn_W_v, L0_attn_W_o, L0_ffn_Wg, L0_ffn_bg, L0_ffn_W1, L0_ffn_b1, L0_ffn_W2, L0_ffn_b2, L1_attn_W_Q, L1_attn_W_K, L1_attn_W_V, L1_attn_W_K_prime, L1_attn_W_O, L1_attn_alpha, L1_ffn_Wqkv, L1_ffn_q_scale, L1_ffn_k_scale, L1_ffn_Wo, L1_ffn_ln_g, L1_ffn_ln_b, L1_ffn_W1, L1_ffn_b1, L1_ffn_W2, L1_ffn_b2):

    def _L0_attn_ref(x, W_q, W_k, W_v, W_o):
        import jax, jax.numpy as jnp
        import numpy as np
        D_MODEL = 128
        N_HEADS = 16
        D_K = 64
        B, S, _ = x.shape
        H, Dk = (N_HEADS, D_K)
        q = (x @ W_q.T).reshape(B, S, H, Dk)
        k = (x @ W_k.T).reshape(B, S, H, Dk)
        v = (x @ W_v.T).reshape(B, S, H, Dk)
        scale = 1.0 / jnp.sqrt(jnp.float32(Dk))
        kv = jnp.einsum('bshd,bshe->bhde', k, v)
        attn = jnp.einsum('bshd,bhde->bshe', q, kv) * scale
        out = attn.reshape(B, S, H * Dk) @ W_o.T
        return out

    def _L0_ffn_ref(x, Wg, bg, W1, b1, W2, b2):
        import jax, jax.numpy as jnp
        import numpy as np
        B, S, D, H, E = (4, 256, 128, 512, 8)
        THRESHOLD = 0.5
        b, s, d = x.shape
        x_flat = x.reshape(-1, d)
        probs = jax.nn.sigmoid(x_flat @ Wg + bg)
        mask = (probs > THRESHOLD).astype(x_flat.dtype)
        weights = probs * mask
        h = jax.nn.relu(jnp.einsum('td,edh->eth', x_flat, W1) + b1[:, None, :])
        expert_out = jnp.einsum('eth,ehd->etd', h, W2) + b2[:, None, :]
        combined = jnp.einsum('te,etd->td', weights, expert_out)
        return combined.reshape(b, s, d)

    def _L1_attn_ref(x, W_Q, W_K, W_V, W_K_prime, W_O, alpha):
        import jax, jax.numpy as jnp
        import numpy as np
        import math
        DIM = 128
        HEADS = 16
        HEAD_DIM = DIM // HEADS
        SCALE = math.sqrt(HEAD_DIM)

        def _heads(y, B, T):
            return y.reshape(B, T, HEADS, HEAD_DIM).transpose(0, 2, 1, 3)
        B, T, C = x.shape
        q = _heads(x @ W_Q.T, B, T)
        k = _heads(x @ W_K.T, B, T)
        v = _heads(x @ W_V.T, B, T)
        kp = _heads(x @ W_K_prime.T, B, T)
        scores = jnp.einsum('bhqd,bhkd->bhqk', q, k) / SCALE
        attn = jax.nn.softmax(scores, axis=-1)
        out_std = jnp.einsum('bhqk,bhkd->bhqd', attn, v)
        scores_p = jnp.einsum('bhqd,bhkd->bhqk', q, kp) / SCALE
        attn_p = jax.nn.softmax(scores_p, axis=-1)
        out_p = jnp.einsum('bhqk,bhkd->bhqd', attn_p, v)
        out = alpha * out_std + (1.0 - alpha) * out_p
        out = out.transpose(0, 2, 1, 3).reshape(B, T, C)
        return out @ W_O.T

    def _L1_ffn_ref(x, Wqkv, q_scale, k_scale, Wo, ln_g, ln_b, W1, b1, W2, b2):
        import jax, jax.numpy as jnp
        import numpy as np
        DIM = 128
        DEPTH = 6
        HEADS = 16
        DIM_HEAD = 64
        WINDOW = 32
        INNER = HEADS * DIM_HEAD
        DIM_INNER = int(DIM * 4 * 2 / 3)
        QK_SCALE = 8.0

        def shift_tokens(t):
            a, s = jnp.split(t, 2, -1)
            s = jnp.pad(s, ((0, 0), (1, 0), (0, 0)))[:, :-1]
            return jnp.concatenate([a, s], -1)

        def l2norm(t):
            return t / jnp.maximum(jnp.linalg.norm(t, axis=-1, keepdims=True), 1e-12)

        def rotate_half(x):
            x1, x2 = jnp.split(x, 2, -1)
            return jnp.concatenate([-x2, x1], -1)

        def rotary_tables(n):
            half = jnp.arange(0, DIM_HEAD, 2, dtype=jnp.float32)
            inv_freq = 1.0 / 10000.0 ** (half / DIM_HEAD)
            t = jnp.arange(n, dtype=jnp.float32)
            freqs = t[:, None] * inv_freq[None, :]
            freqs = jnp.concatenate([freqs, freqs], -1)
            base_scale = (half + 0.4 * DIM_HEAD) / (1.4 * DIM_HEAD)
            power = (t - n // 2) / (WINDOW // 2)
            scale = base_scale[None, :] ** power[:, None]
            scale = jnp.concatenate([scale, scale], -1)
            return (freqs, scale)

        def local_attention(q, k, v):
            b, h, n, d = q.shape
            w = WINDOW
            nw = n // w
            bq = q.reshape(b, h, nw, w, d)
            bk = k.reshape(b, h, nw, w, d)
            bv = v.reshape(b, h, nw, w, d)

            def look(t):
                p = jnp.pad(t, ((0, 0), (0, 0), (1, 0), (0, 0), (0, 0)))
                return jnp.concatenate([p[:, :, :nw], p[:, :, 1:]], axis=3)
            bk2, bv2 = (look(bk), look(bv))
            seq = jnp.arange(n).reshape(nw, w)
            seq_p = jnp.pad(seq, ((1, 0), (0, 0)), constant_values=-1)
            jt = jnp.concatenate([seq_p[:nw], seq_p[1:]], axis=1)
            it = seq[:, :, None]
            jb = jt[:, None, :]
            mask = (it < jb) | (it > jb + w) | (jb == -1)
            sim = jnp.einsum('bhwie,bhwje->bhwij', bq, bk2) * QK_SCALE
            sim = jnp.where(mask, -jnp.finfo(sim.dtype).max, sim)
            attn = jax.nn.softmax(sim, -1)
            out = jnp.einsum('bhwij,bhwje->bhwie', attn, bv2)
            return out.reshape(b, h, n, d)

        def attn_layer(x, Wqkv, qs, ksc, Wo):
            b, n, _ = x.shape
            qkv = x @ Wqkv
            q, k, v = jnp.split(qkv, 3, -1)
            sh = lambda t: t.reshape(b, n, HEADS, DIM_HEAD).transpose(0, 2, 1, 3)
            q, k, v = (sh(q), sh(k), sh(v))
            q = l2norm(q) * qs
            k = l2norm(k) * ksc
            freqs, scale = rotary_tables(n)
            cos, sin = (jnp.cos(freqs), jnp.sin(freqs))
            q = q * cos * scale + rotate_half(q) * sin * scale
            inv = 1.0 / scale
            k = k * cos * inv + rotate_half(k) * sin * inv
            out = local_attention(q, k, v)
            out = out.transpose(0, 2, 1, 3).reshape(b, n, INNER)
            return out @ Wo

        def ffn_layer(x, g, bln, W1, b1, W2, b2):
            mu = x.mean(-1, keepdims=True)
            var = ((x - mu) ** 2).mean(-1, keepdims=True)
            xn = (x - mu) / jnp.sqrt(var + 1e-05) * g + bln
            hg = xn @ W1 + b1
            a, gate = jnp.split(hg, 2, -1)
            return a * jax.nn.gelu(gate, approximate=False) @ W2 + b2
        for i in range(DEPTH):
            x = attn_layer(shift_tokens(x), Wqkv[i], q_scale[i], k_scale[i], Wo[i]) + x
            x = ffn_layer(shift_tokens(x), ln_g[i], ln_b[i], W1[i], b1[i], W2[i], b2[i]) + x
        return x
    x = L0_attn_x
    x = x + 0.5 * _L0_ffn_ref(_layernorm(x, axis=-1), L0_ffn_Wg, L0_ffn_bg, L0_ffn_W1, L0_ffn_b1, L0_ffn_W2, L0_ffn_b2)
    x = x + _L0_attn_ref(_layernorm(x, axis=-1), L0_attn_W_q, L0_attn_W_k, L0_attn_W_v, L0_attn_W_o)
    x = x + 0.5 * _L0_ffn_ref(_layernorm(x, axis=-1), L0_ffn_Wg, L0_ffn_bg, L0_ffn_W1, L0_ffn_b1, L0_ffn_W2, L0_ffn_b2)
    x = x + 0.5 * _L1_ffn_ref(_layernorm(x, axis=-1), L1_ffn_Wqkv, L1_ffn_q_scale, L1_ffn_k_scale, L1_ffn_Wo, L1_ffn_ln_g, L1_ffn_ln_b, L1_ffn_W1, L1_ffn_b1, L1_ffn_W2, L1_ffn_b2)
    x = x + _L1_attn_ref(_layernorm(x, axis=-1), L1_attn_W_Q, L1_attn_W_K, L1_attn_W_V, L1_attn_W_K_prime, L1_attn_W_O, L1_attn_alpha)
    x = x + 0.5 * _L1_ffn_ref(_layernorm(x, axis=-1), L1_ffn_Wqkv, L1_ffn_q_scale, L1_ffn_k_scale, L1_ffn_Wo, L1_ffn_ln_g, L1_ffn_ln_b, L1_ffn_W1, L1_ffn_b1, L1_ffn_W2, L1_ffn_b2)
    return x

_drawn_inputs = setup_inputs


def setup_inputs(seed=0):
    import zlib

    import numpy as np

    out = dict(_drawn_inputs(seed))
    spreads = {'L1_ffn_q_scale': (1.0, 0.6),
     'L1_ffn_k_scale': (1.0, 0.6),
     'L1_ffn_ln_g': (1.0, 0.6),
     'L1_ffn_ln_b': (0.0, 0.8),
     'L1_ffn_b1': (0.0, 0.8),
     'L1_ffn_b2': (0.0, 0.1)}
    factors = {'L1_attn_W_Q': 8.0,
     'L1_attn_W_K': 8.0,
     'L1_attn_W_V': 8.0,
     'L1_attn_W_K_prime': 8.0,
     'L1_attn_W_O': 8.0,
     'L1_ffn_W1': 3.331,
     'L1_ffn_W2': 3.251}
    for name, (base, spread) in spreads.items():
        noise = np.random.default_rng([zlib.crc32(name.encode()), seed]).standard_normal(out[name].shape)
        drawn = base * np.exp(spread * noise) if base else spread * noise
        out[name] = jnp.asarray(drawn.astype(out[name].dtype))
    for name, factor in factors.items():
        out[name] = (out[name] * factor).astype(out[name].dtype)
    return out
```

```python
from contextlib import ExitStack

import numpy as np

import concourse.bass as bass
from concourse import mybir

ALU = mybir.AluOpType
ACT = mybir.ActivationFunctionType
AX_X = mybir.AxisListType.X
F32 = mybir.dt.float32
BF16 = mybir.dt.bfloat16

P = 128
D = 128
SEQS, T = 4, 512
TILES = T // P
NTOK = SEQS * T
LN_EPS = 1e-5
EXPERTS, HID = 8, 512
HBLK = HID // P
LIN_HEADS, LIN_DK = 16, 64
DEPTH, HEADS, DH, WINDOW = 6, 16, 64, 32
INNER = HEADS * DH
PAIRS = HEADS // 2
GROUPS = HEADS // 4
KEYS = P + WINDOW
FF = int(D * 4 * 2 / 3)
FBLK = -(-FF // P)
QK_SCALE = 8.0
MASKED = -1.0e30
AH, AD = 16, 8
SPLITS = 3
STACK = SPLITS * SPLITS * AD
CREDIT = 2
ds = bass.ds


def blk(k):
    return min(P, FF - k * P)


class Shared:
    pass


def sem_start(eng, sems):
    for s, per_tile in sems:
        eng.sem_inc(s, CREDIT * per_tile + 1)


NEWTON = 11


def inverse_sqrt(dve, step, done, src, x, y, t, op, guard):
    i32 = mybir.dt.int32
    dve.tensor_scalar(x, src, guard, None, op).then_inc(step, 1)
    dve.wait_ge(step, done + 1)
    dve.tensor_scalar(y.bitcast(i32), x.bitcast(i32), -0.5, float(0x5F3759DF), ALU.mult, ALU.add).then_inc(step, 1)
    for k in range(3):
        dve.wait_ge(step, done + (3 * k + 2))
        dve.tensor_tensor(t, y, y, ALU.mult).then_inc(step, 1)
        dve.wait_ge(step, done + (3 * k + 3))
        dve.scalar_tensor_tensor(out=t, in0=t, scalar=-0.5, in1=x, op0=ALU.mult, op1=ALU.mult).then_inc(step, 1)
        dve.wait_ge(step, done + (3 * k + 4))
        dve.scalar_tensor_tensor(out=y, in0=t, scalar=1.5, in1=y, op0=ALU.add, op1=ALU.mult).then_inc(step, 1)


def stage_semaphores(nc, ctx, stage):
    used = []
    ctx.callback(nc.all_engine_barrier)
    ctx.callback(nc.clear_and_free_semaphores, used)

    def sem(name):
        used.append(nc.alloc_semaphore(f"{stage}_{name}"))
        return used[-1]
    return sem


def layernorm_block(nc, M, src, dst, name):
    with ExitStack() as ctx:
        sem = stage_semaphores(nc, ctx, name)
        sb = lambda n, s: ctx.enter_context(nc.sbuf_tensor(f"{name}_{n}", s, F32))
        mean_full, centred, squared, var_full, step, rstd_full, out_ready = (
            sem(n) for n in ("mean_full", "centred", "squared", "var_full", "step", "rstd_full", "out_ready"))
        sq = sb("sq", [P, 2, T])
        var, rstd, tmp = (sb(n, [P, SEQS, TILES]) for n in ("var", "rstd", "tmp"))
        block = ctx.enter_context(nc.Block())
        MEAN, VAR, RSTD = M.bank[0:2], M.bank[2:4], M.bank[4:6]

        @block.tensor
        def _(pe):
            def spread(s):
                pe.wait_ge(step, NEWTON * (s + 1))
                if s >= 2:
                    pe.wait_ge(out_ready, s - 1)
                for i in range(TILES):
                    mm = pe.matmul(RSTD[s % 2][:, i * P:(i + 1) * P], rstd[:, s, i:i + 1].broadcast_to([P, P]),
                                   M.ident[:, :], start=True, stop=True)
                mm.then_inc(rstd_full, 1)

            for s in range(SEQS):
                if s >= 2:
                    pe.wait_ge(centred, s - 1)
                pe.matmul(MEAN[s % 2][:, :], M.mean_w[:, :], src[:, s * T:(s + 1) * T],
                          start=True, stop=True).then_inc(mean_full, 1)
            for s in range(SEQS):
                pe.wait_ge(squared, s + 1)
                if s >= 2:
                    pe.wait_ge(step, NEWTON * (s - 1))
                for i in range(TILES):
                    mm = pe.matmul(VAR[s % 2][:, i:i + 1], sq[:, s % 2, i * P:(i + 1) * P], M.mean_w[:, 0:1],
                                   start=True, stop=True)
                mm.then_inc(var_full, 1)
                if s >= 1:
                    spread(s - 1)
            spread(SEQS - 1)

        @block.scalar
        def _(act):
            for s in range(SEQS):
                act.wait_ge(centred, s + 1)
                if s >= 2:
                    act.wait_ge(var_full, s - 1)
                act.activation(sq[:, s % 2, :], dst[:, s * T:(s + 1) * T], ACT.Square).then_inc(squared, 1)

        @block.vector
        def _(dve):
            def scale(s):
                dve.wait_ge(rstd_full, s + 1)
                dve.tensor_tensor(dst[:, s * T:(s + 1) * T], dst[:, s * T:(s + 1) * T], RSTD[s % 2][:, :],
                                  ALU.mult).then_inc(out_ready, 1)

            for s in range(SEQS):
                dve.wait_ge(mean_full, s + 1)
                dve.tensor_tensor(dst[:, s * T:(s + 1) * T], src[:, s * T:(s + 1) * T], MEAN[s % 2][:, :],
                                  ALU.subtract).then_inc(centred, 1)
            for s in range(SEQS):
                dve.wait_ge(var_full, s + 1)
                inverse_sqrt(dve, step, NEWTON * s, VAR[s % 2][:, 0:TILES], var[:, s, :], rstd[:, s, :], tmp[:, s, :],
                             ALU.add, LN_EPS)
                if s >= 1:
                    scale(s - 1)
            scale(SEQS - 1)


def expert_block(nc, M, W, name):
    UNITS = 2 * SEQS
    with ExitStack() as ctx:
        sem = stage_semaphores(nc, ctx, name)
        sb = lambda n, s, d=F32: ctx.enter_context(nc.sbuf_tensor(f"{name}_{n}", s, d))
        logits_full, logits_ready, prob_ready, gate_ready, gate_t_full, gate_t_ready = (
            sem(n) for n in ("logits_full", "logits_ready", "prob_ready", "gate_ready", "gate_t_full", "gate_t_ready"))
        passed = sem("passed")
        hid_full, relu_dve, relu_act, out_full, combined = (
            sem(n) for n in ("hid_full", "relu_dve", "relu_act", "out_full", "combined"))
        bias_full, bias_copied, back_full, x_updated = (
            sem(n) for n in ("bias_full", "bias_copied", "back_full", "x_updated"))
        loaded = [sem("loaded0"), sem("loaded1")]
        w1 = sb("w1", [P, 2, HID])
        w2 = sb("w2", [P, 2, HBLK, D])
        logit, prob, gate = (sb(n, [P, NTOK // P, EXPERTS]) for n in ("logit", "prob", "gate"))
        gate_t = sb("gate_t", [EXPERTS, NTOK])
        hid = sb("hid", [P, 2, HBLK, T])
        acc = sb("acc", [P, NTOK // P, D])
        block = ctx.enter_context(nc.Block())
        HB, YB, GB = M.bank[0:4], M.bank[4:6], M.bank[6:8]
        gate_cols = gate[:, :, :].rearrange("p t e -> p (t e)")

        @block.sync
        def _(sp):
            with sp.Fori(0, EXPERTS // 2) as e2:
                for u in range(2):
                    sp.wait_ge(out_full, e2 * UNITS + (u * SEQS + 2 - (SEQS if u else 0)))
                    sp.dma_start(w1[:, u, :], W["moe_w1"][:, ds(e2 * (2 * HID) + u * HID, HID)]).then_inc(loaded[u], 16)
                    sp.dma_start(w2[:, u, :, :], W["moe_w2"][:, ds(e2 * (2 * HBLK * D) + u * HBLK * D, HBLK * D)]
                                 .rearrange("p (k d) -> p k d", d=D)).then_inc(loaded[u], 16)

        @block.tensor
        def _(pe):
            pe.wait_ge(M.moe_loaded, 16 * M.moe_dmas)
            for t in range(NTOK // P):
                mm = pe.matmul(GB[0][:, t * EXPERTS:(t + 1) * EXPERTS], M.xh[:, t * P:(t + 1) * P], M.wg[:, :],
                               start=True, stop=True)
            mm.then_inc(logits_full, 1)
            pe.wait_ge(gate_ready, 1)
            for s in range(SEQS):
                for i in range(TILES):
                    mm = pe.transpose(HB[s][0:EXPERTS, i * P:(i + 1) * P], gate[:, s * TILES + i, :], M.ident[:, :])
                mm.then_inc(gate_t_full, 1)
            for s in range(SEQS):
                pe.wait_ge(gate_t_ready, s + 1)
                if s >= 2:
                    pe.wait_ge(bias_copied, s - 1)
                for i in range(TILES):
                    mm = pe.matmul(GB[s % 2][:, i * D:(i + 1) * D], gate_t[:, s * T + i * P:s * T + (i + 1) * P], M.b2[:, :],
                                   start=True, stop=True)
                mm.then_inc(bias_full, 1)
            with pe.Fori(0, EXPERTS // 2) as e2:
                def first(u, v, h):
                    for k in range(HBLK):
                        n = 2 * (u * SEQS + v) + k // 2 + 1
                        pe.wait_ge(relu_act if k % 2 else relu_dve, e2 * (2 * UNITS) + n)
                        pe.matmul(HB[k][:, :], w1[:, u, k * P:(k + 1) * P], M.xh[:, v * T:(v + 1) * T],
                                  start=True, stop=True).then_inc(hid_full, 1)

                def second(u, v, h):
                    n = u * SEQS + v
                    pe.wait_ge(relu_dve, e2 * (2 * UNITS) + (2 * n + 4))
                    pe.wait_ge(relu_act, e2 * (2 * UNITS) + (2 * n + 4))
                    pe.wait_ge(combined, e2 * UNITS + (n + 1))
                    for i in range(TILES):
                        for k in range(HBLK):
                            mm = pe.matmul(YB[h][:, i * D:(i + 1) * D], hid[:, h, k, i * P:(i + 1) * P], w2[:, u, k, :],
                                           start=(k == 0), stop=(k == HBLK - 1))
                    mm.then_inc(out_full, 1)

                for u in range(2):
                    pe.wait_ge(loaded[u], e2 * 32 + 32)
                    for v in range(0, SEQS, 2):
                        first(u, v, 0)
                        first(u, v + 1, 1)
                        second(u, v, 0)
                        second(u, v + 1, 1)
            pe.wait_ge(combined, EXPERTS * SEQS + 2)
            for s in range(SEQS):
                for i in range(TILES):
                    mm = pe.transpose(HB[s][:, i * P:(i + 1) * P], acc[:, s * TILES + i, :], M.ident[:, :])
                mm.then_inc(back_full, 1)

        @block.scalar
        def _(act):
            act.sem_inc(relu_act, 2)
            act.wait_ge(logits_ready, 1)
            act.activation(prob[:, :, :], logit[:, :, :], ACT.Sigmoid).then_inc(prob_ready, 1)
            with act.Fori(0, EXPERTS // 2) as e2:
                for n in range(UNITS):
                    act.wait_ge(out_full, e2 * UNITS + (n + 1))
                    for k in (1, 3):
                        act.wait_ge(hid_full, e2 * (UNITS * HBLK) + (n * HBLK + k + 1))
                        act.sem_inc(passed, 1)
                        act.activation(hid[:, n % 2, k, :], HB[k][:, :], ACT.Relu,
                                       bias=M.b1[:, ds(e2 * (2 * HBLK) + (n // SEQS * HBLK + k), 1)]).then_inc(relu_act, 1)

        @block.vector
        def _(dve):
            dve.sem_inc(relu_dve, 2)
            dve.sem_inc(out_full, 2)
            dve.sem_inc(combined, 2)
            dve.wait_ge(logits_full, 1)
            dve.tensor_tensor(logit[:, :, :], GB[0][:, 0:NTOK // P * EXPERTS].rearrange("p (t e) -> p t e", e=EXPERTS),
                              M.bg[:, :].rearrange("p (o e) -> p o e", o=1).broadcast_to([P, NTOK // P, EXPERTS]),
                              ALU.add).then_inc(logits_ready, 1)
            dve.wait_ge(prob_ready, 1)
            dve.scalar_tensor_tensor(out=gate[:, :, :], in0=logit[:, :, :], scalar=0.0, in1=prob[:, :, :],
                                     op0=ALU.is_gt, op1=ALU.mult).then_inc(gate_ready, 1)
            for s in range(SEQS):
                dve.wait_ge(gate_t_full, s + 1)
                dve.tensor_copy(gate_t[:, s * T:(s + 1) * T], HB[s][0:EXPERTS, :]).then_inc(gate_t_ready, 1)
            for s in range(SEQS):
                dve.wait_ge(bias_full, s + 1)
                dve.tensor_copy(acc[:, s * TILES:(s + 1) * TILES, :],
                                GB[s % 2][:, :].rearrange("p (i d) -> p i d", d=D)).then_inc(bias_copied, 1)
            dve.wait_ge(bias_copied, SEQS)
            with dve.Fori(0, EXPERTS // 2) as e2:
                def relu(n):
                    dve.wait_ge(out_full, e2 * UNITS + (n + 1))
                    for k in (0, 2):
                        dve.wait_ge(hid_full, e2 * (UNITS * HBLK) + (n * HBLK + k + 1))
                        dve.tensor_scalar(hid[:, n % 2, k, :], HB[k][:, :],
                                          M.b1[:, ds(e2 * (2 * HBLK) + (n // SEQS * HBLK + k), 1)], 0.0,
                                          ALU.add, ALU.max).then_inc(relu_dve, 1)

                def combine(n):
                    dve.wait_ge(out_full, e2 * UNITS + (n + 3))
                    dve.wait_ge(combined, e2 * UNITS + (n + 2))
                    for i in range(TILES):
                        t = n % SEQS * TILES + i
                        last = dve.scalar_tensor_tensor(
                            out=acc[:, t, :], in0=YB[n % 2][:, i * D:(i + 1) * D],
                            scalar=gate_cols[:, ds(e2 * 2 + (t * EXPERTS + n // SEQS), 1)],
                            in1=acc[:, t, :], op0=ALU.mult, op1=ALU.add)
                    last.then_inc(combined, 1)

                for n in range(0, UNITS, 2):
                    relu(n)
                    relu(n + 1)
                    combine(n)
                    combine(n + 1)
            for s in range(SEQS):
                dve.wait_ge(back_full, s + 1)
                dve.scalar_tensor_tensor(out=M.x[:, s * T:(s + 1) * T], in0=HB[s][:, :], scalar=0.5,
                                         in1=M.x[:, s * T:(s + 1) * T], op0=ALU.mult, op1=ALU.add).then_inc(x_updated, 1)


def linear_attention_block(nc, M):
    with ExitStack() as ctx:
        sem = stage_semaphores(nc, ctx, "lin")
        sb = lambda n, s, d=F32: ctx.enter_context(nc.sbuf_tensor(f"lin_{n}", s, d))
        qk_full, vo_full, tok_full, tok_copied, copied_qk, copied_vo = (
            sem(n) for n in ("qk_full", "vo_full", "tok_full", "tok_copied", "copied_qk", "copied_vo"))
        gram_full, gram_copied, gvo_full, gvo_copied, mix_full, mix_copied, out_full, x_updated = (
            sem(n) for n in ("gram_full", "gram_copied", "gvo_full", "gvo_copied", "mix_full", "mix_copied",
                             "out_full", "x_updated"))
        HP = LIN_HEADS // 2
        qk = sb("qk", [P, LIN_HEADS * D])
        vo = sb("vo", [P, LIN_HEADS * D])
        tok = sb("tok", [P, NTOK // P, D])
        gram = sb("gram", [P, SEQS * D])
        gvo = sb("gvo", [P, LIN_HEADS, SEQS, D])
        mix = sb("mix", [P, SEQS * D])
        block = ctx.enter_context(nc.Block())
        B = M.bank

        @block.tensor
        def _(pe):
            pe.wait_ge(M.lin_loaded, 16 * M.lin_dmas)
            for j in range(2):
                for c in range(2):
                    for n in range(4):
                        p_ = 4 * c + n
                        mm = pe.matmul(B[2 * j + c][:, n * D:(n + 1) * D], M.wk[64 * j:64 * j + 64, p_ * D:(p_ + 1) * D],
                                       M.wq[64 * j:64 * j + 64, p_ * D:(p_ + 1) * D], start=True, stop=True)
                    mm.then_inc(qk_full, 1)
            for j in range(2):
                for c in range(2):
                    for n in range(4):
                        p_ = 4 * c + n
                        mm = pe.matmul(B[4 + 2 * j + c][:, n * D:(n + 1) * D], M.wv[64 * j:64 * j + 64, p_ * D:(p_ + 1) * D],
                                       M.wo_lin[64 * j:64 * j + 64, p_ * D:(p_ + 1) * D], start=True, stop=True)
                    mm.then_inc(vo_full, 1)
            for s in range(SEQS):
                pe.wait_ge(copied_qk, s + 1)
                for i in range(TILES):
                    mm = pe.transpose(B[s][:, i * P:(i + 1) * P], M.xh[:, (s * TILES + i) * P:(s * TILES + i + 1) * P],
                                      M.ident[:, :])
                mm.then_inc(tok_full, 1)
            pe.wait_ge(copied_vo, 1)
            for s in range(SEQS):
                pe.wait_ge(tok_copied, s + 1)
                for i in range(TILES):
                    mm = pe.matmul(B[4][:, s * D:(s + 1) * D], tok[:, s * TILES + i, :], tok[:, s * TILES + i, :],
                                   start=(i == 0), stop=(i == TILES - 1))
            mm.then_inc(gram_full, 1)
            pe.wait_ge(gram_copied, 1)
            pe.wait_ge(copied_vo, 4)
            for s in range(SEQS):
                for c in range(4):
                    n = 4 * s + c
                    if n >= 4:
                        pe.wait_ge(gvo_copied, n - 3)
                    pe.matmul(B[n % 4][:, :], gram[:, s * D:(s + 1) * D], vo[:, c * T:(c + 1) * T],
                              start=True, stop=True).then_inc(gvo_full, 1)
            pe.wait_ge(gvo_copied, 16)
            for h in range(LIN_HEADS):
                mm = pe.matmul(B[5][:, :], qk[:, h * D:(h + 1) * D], gvo[:, h, :, :].rearrange("p s d -> p (s d)"),
                               start=(h == 0), stop=(h == LIN_HEADS - 1))
            mm.then_inc(mix_full, 1)
            pe.wait_ge(mix_copied, 1)
            for s in range(SEQS):
                pe.matmul(B[s][:, :], mix[:, s * D:(s + 1) * D], M.xh[:, s * T:(s + 1) * T],
                          start=True, stop=True).then_inc(out_full, 1)

        @block.scalar
        def _(act):
            for n in range(4):
                act.wait_ge(vo_full, n + 1)
                act.activation(vo[:, n * T:(n + 1) * T], B[4 + n][:, :], ACT.Copy).then_inc(copied_vo, 1)
            for n in range(0, 16):
                s, c = n // 4, n % 4
                act.wait_ge(gvo_full, n + 1)
                act.activation(gvo[:, 4 * c:4 * c + 4, s, :], B[n % 4][:, :].rearrange("p (h d) -> p h d", d=D),
                               ACT.Copy).then_inc(gvo_copied, 1)

        @block.vector
        def _(dve):
            for n in range(4):
                dve.wait_ge(qk_full, n + 1)
                dve.tensor_copy(qk[:, n * T:(n + 1) * T], B[n][:, :]).then_inc(copied_qk, 1)
            for s in range(SEQS):
                dve.wait_ge(tok_full, s + 1)
                dve.tensor_copy(tok[:, s * TILES:(s + 1) * TILES, :],
                                B[s][:, :].rearrange("p (i d) -> p i d", d=D)).then_inc(tok_copied, 1)
            dve.wait_ge(gram_full, 1)
            dve.tensor_copy(gram[:, :], B[4][:, :]).then_inc(gram_copied, 1)
            dve.wait_ge(mix_full, 1)
            dve.tensor_scalar(mix[:, :], B[5][:, :], LIN_DK ** -0.5, None, ALU.mult).then_inc(mix_copied, 1)
            for s in range(SEQS):
                dve.wait_ge(out_full, s + 1)
                dve.tensor_tensor(M.x[:, s * T:(s + 1) * T], M.x[:, s * T:(s + 1) * T], B[s][:, :],
                                  ALU.add).then_inc(x_updated, 1)


def local_transformer_block(nc, M, W, name):
    with ExitStack() as ctx:
        sem = stage_semaphores(nc, ctx, name)
        sb = lambda n, s, d=F32: ctx.enter_context(nc.sbuf_tensor(f"{name}_{n}", s, d))
        proj_full, squared, v_ready, rotated, qk_ready, turned_full, turned_ready = (
            sem(n) for n in ("proj_full", "squared", "v_ready", "rotated", "qk_ready", "turned_full", "turned_ready"))
        score_full, max_ready, exp_done, recip_ready, prob_ready, pt_full, pt_ready = (
            sem(n) for n in ("score_full", "max_ready", "exp_done", "recip_ready", "prob_ready", "pt_full", "pt_ready"))
        out_full, out_ready, y_full, z_attn = (sem(n) for n in ("out_full", "out_ready", "y_full", "z_attn"))
        passed, pe_passed = sem("passed"), sem("pe_passed")
        prev_loaded = [sem("prev_loaded_even"), sem("prev_loaded_odd")]
        xa_first, xa_rest, shifted_ffn, tables_ready, norm_step, sum_ready = (
            sem(n) for n in ("xa_first", "xa_rest", "shifted_ffn", "tables_ready", "norm_step", "sum_ready"))
        mean_full, centred, sqf_ready, var_full, rstd_step, rstd_full, xn_scaled, xn_ready = (
            sem(n) for n in ("mean_full", "centred", "sqf_ready", "var_full", "rstd_step", "rstd_full",
                             "xn_scaled", "xn_ready"))
        gate_full, gelu_done, lin_full, hid_ready, ffn_full, z_ffn = (
            sem(n) for n in ("gate_full", "gelu_done", "lin_full", "hid_ready", "ffn_full", "z_ffn"))
        qkv_loaded, rest_loaded, vec_loaded, cleared, x_added = (
            sem(n) for n in ("qkv_loaded", "rest_loaded", "vec_loaded", "cleared", "x_added"))

        z = M.z
        xa = sb("xa", [P, T])
        xs = sb("xs", [P, SEQS * T])
        wqkv = sb("wqkv", [P, 3 * INNER])
        wo = sb("wo", [P, PAIRS * D])
        w1 = sb("w1", [P, 2 * FF])
        w2 = sb("w2", [P, FBLK * D])
        vec = sb("vec", [P, 3 * FBLK])
        scales = sb("scales", [P, 4, DH])
        rot = sb("rot", [P, 4, TILES, DH])
        sq = sb("sq", [P, 2, T])
        rc = sb("rc", [P, 2, T])
        rs = sb("rs", [P, 2, T])
        qk = sb("qk", [P, 2, T])
        ssq = sb("ssq", [P, 2, 8])
        rn = sb("rn", [P, 2, 8])
        rt = sb("rt", [P, 2, 8])
        qT = sb("qT", [P, 2, PAIRS, 2, P])
        kT = sb("kT", [P, PAIRS, WINDOW + T])
        V = sb("V", [P, 2, INNER])
        Vp = sb("Vp", [P, 2, PAIRS, P])
        negmax = sb("negmax", [P, 4, 2])
        total = sb("total", [P, 4, 2])
        recip = sb("recip", [P, 4, 2])
        prob = sb("prob", [P, 2, 4, KEYS])
        prob_prev = sb("prob_prev", [P, 2, 4, WINDOW])
        PT = sb("PT", [P, 2, 4, P])
        PTp = sb("PTp", [P, 2, P])
        outT = sb("outT", [P, PAIRS, P])
        xc = sb("xc", [P, 2, T])
        var, rstd, vt = (sb(n, [P, 2, TILES]) for n in ("var", "rstd", "vt"))
        xn = sb("xn", [P, 2, T])
        gg = sb("gg", [P, FBLK, T])
        hid = sb("hid", [P, FBLK, T])
        block = ctx.enter_context(nc.Block())
        PJ, TQ, SC, PTB, PX, OT = M.bank[0:2], M.bank[2], M.bank[3:5], M.bank[5], M.bank[6], M.bank[7]

        def at(n, per_tile, tile, k):
            return n * (TILES * per_tile) + (tile * per_tile + k + CREDIT * per_tile + 1)

        def prev_count(n, j):
            return n * (64 * ((TILES - 1 + j % 2) // 2)) + 64 * ((j + 1) // 2)

        PROJ = ["k0", "q0", "v0", "k1", "q1", "v1"]
        ROT = ["k0", "q0", "k1", "q1"]
        COL = {"q": 0, "k": INNER, "v": 2 * INNER}
        PLAN = [["k0", "q0"], ["v0", "k1"], ["Tk0", "q1", "v1"], ["Tq0", "Tk1", "Tq1"]]
        PLAN_LAST = [["k0"], ["q0"], ["v0", "k1"], ["Tk0", "q1"], ["Tq0", "v1"], ["Tk1"], ["Tq1"]]
        PROLOGUE = ["k0", "q0", "v0", "k1", "Tk0", "q1", "v1", "Tq0", "Tk1", "Tq1"]

        def schedule(last):
            slots = [(i, g) for i in range(TILES) for g in range(GROUPS)]
            for n in range(len(slots) + 3):
                now = slots[n] if n < len(slots) else None
                if n < 12:
                    pieces, nxt = PLAN[n % 4], n // 4 + 1
                else:
                    pieces, nxt = ([] if last else PLAN_LAST[n - 12]), TILES
                value = slots[n - 2] if 2 <= n < len(slots) + 2 else None
                turn = slots[n - 1] if 1 <= n <= len(slots) else None
                y = slots[n - 2][0] if value and slots[n - 2][1] == GROUPS - 1 else None
                yield now, value, pieces, nxt, turn, y

        def sequences(eng, layer, body):
            with eng.Fori(0, SEQS - 1) as s:
                body(s, layer * SEQS + s, False)
            body(SEQS - 1, layer * SEQS + (SEQS - 1), True)

        @block.sync
        def _(sp):
            with sp.Fori(0, DEPTH) as L:
                sp.wait_ge(proj_full, at(L * SEQS, 6, -1, 6))
                sp.dma_start(wqkv[:, :], W["wqkv"][ds(L, 1), :, :].rearrange("o p n -> p (o n)")).then_inc(qkv_loaded, 16)
                sp.wait_ge(tables_ready, L * 4 + 1)
                sp.dma_start(scales[:, :, :],
                             W["scales"][ds(L, 1), :].broadcast_to([P, 4 * DH]).rearrange("p (a d) -> p a d", d=DH)
                             ).then_inc(qkv_loaded, 16)
                sp.wait_ge(z_ffn, L * SEQS + 1)
                sp.dma_start(wo[:, :], W["wo"][ds(L, 1), :, :].rearrange("o p n -> p (o n)")).then_inc(rest_loaded, 16)
                sp.dma_start(w1[:, :], W["w1"][ds(L, 1), :, :].rearrange("o p n -> p (o n)")).then_inc(rest_loaded, 16)
                sp.dma_start(w2[:, :], W["w2"][ds(L, 1), :, :].rearrange("o p n -> p (o n)")).then_inc(rest_loaded, 16)
                sp.dma_start(vec[:, :], W["vec"][ds(L, 1), :, :].rearrange("o p n -> p (o n)")).then_inc(rest_loaded, 16)
                with sp.Fori(0, SEQS) as s:
                    n = L * SEQS + s
                    for j in range(TILES - 1):
                        sp.wait_ge(v_ready, at(n, 2, j, 2))
                        sp.sem_inc(passed, 1)
                        sp.wait_ge(out_full, at(n, 4, j - 1, 4))
                        for r in range(4):
                            e, c = r // 2, r % 2
                            src = V[P - WINDOW:P, j % 2, :].rearrange("p (q e c d) -> p q e c d", e=2, c=2, d=DH)[:, :, e, c, :]
                            dst = Vp[32 * r:32 * r + 32, (j + 1) % 2, :, :].rearrange(
                                "p (q e) (c d) -> p q e c d", e=2, c=2)[:, :, e, c, :]
                            sp.dma_start(dst, src).then_inc(prev_loaded[(j + 1) % 2], 16)

        @block.tensor
        def _(pe):
            def proj(n, j, what, s):
                idx = PROJ.index(what)
                if idx == 0:
                    pe.wait_ge(rotated, at(n, 4, j - 1, 4))
                elif idx == 1:
                    pe.wait_ge(v_ready, at(n, 2, j - 1, 2))
                elif idx == 4:
                    pe.wait_ge(v_ready, at(n, 2, j, 1))
                else:
                    pe.wait_ge(rotated, at(n, 4, j, {2: 1, 3: 2, 5: 3}[idx]))
                col = COL[what[0]] + int(what[1]) * T
                pe.matmul(PJ[idx % 2][:, :], xa[:, j % TILES * P:(j % TILES + 1) * P], wqkv[:, col:col + T],
                          start=True, stop=True).then_inc(proj_full, 1)

            def turn_qk(n, j, what):
                f = ROT.index(what[1:])
                pe.wait_ge(qk_ready, at(n, 4, j, f + 1))
                pe.wait_ge(turned_ready, at(n, 4, j, f))
                for c in range(4):
                    mm = pe.transpose(TQ[:, c * P:(c + 1) * P], qk[:, f % 2, c * P:(c + 1) * P], M.ident[:, :])
                mm.then_inc(turned_full, 1)

            def pieces(n, j, todo, s):
                for what in todo:
                    if what[0] == "T":
                        turn_qk(n, j, what)
                    else:
                        if what == "k0" and j == TILES:
                            pe.wait_ge(xa_first, n + 2)
                        if what == "k0" and j == 1:
                            pe.wait_ge(xa_rest, n + 1)
                        proj(n, j, what, s)

            def scores(n, j, p):
                if p == 0:
                    pe.wait_ge(turned_ready, at(n, 4, j, 2))
                if p == PAIRS // 2:
                    pe.wait_ge(turned_ready, at(n, 4, j, 4))
                pe.wait_ge(exp_done, at(n, 8, j, p - 1))
                bank = SC[p % 2]
                pe.matmul(bank[:, 0:2 * KEYS], M.ident16[:, :], M.mask[:, int(j > 0), :],
                          start=True, stop=False, skip_group_check=True)
                for c in range(2):
                    mm = pe.matmul(bank[:, c * KEYS:(c + 1) * KEYS], qT[:, j % 2, p, c, :], kT[:, p, j * P:j * P + KEYS],
                                   start=False, stop=(c == 1), skip_group_check=True)
                mm.then_inc(score_full, 1)

            def turn_probs(n, j, g):
                pe.wait_ge(prob_ready, at(n, 8, j, 2 * g + 2))
                pe.wait_ge(pt_ready, at(n, 4, j, g))
                for h in range(4):
                    pe.transpose(PTB[:, h * P:(h + 1) * P], prob[:, g % 2, h, WINDOW:KEYS], M.ident[:, :])
                pe.transpose(PX[:, 0:P], prob_prev[:, g % 2, :, :].rearrange("p h k -> p (h k)"), M.ident[:, :]).then_inc(pt_full, 1)

            def values(n, j, g):
                pe.wait_ge(pt_ready, at(n, 4, j, g + 1))
                if g == 0:
                    pe.wait_ge(z_attn, at(n, 1, j - 1, 1))
                    if j > 0:
                        pe.wait_ge(prev_loaded[j % 2], prev_count(n, j))
                else:
                    pe.wait_ge(out_ready, at(n, 4, j, g))
                if g % 2 == 0:
                    pe.wait_ge(v_ready, at(n, 2, j, g // 2 + 1))
                for pp in range(2):
                    p = 2 * g + pp
                    pe.matmul(OT[:, pp * P:(pp + 1) * P], Vp[:, j % 2, p, :], PTp[:, g % 2, :],
                              start=True, stop=False, skip_group_check=True)
                    for c in range(2):
                        mm = pe.matmul(OT[64 * c:64 * c + 64, pp * P:(pp + 1) * P],
                                       V[:, j % 2, (2 * p + c) * DH:(2 * p + c + 1) * DH],
                                       PT[:, g % 2, 2 * pp + c, :], start=False, stop=True, skip_group_check=True)
                mm.then_inc(out_full, 1)

            def output(n, j):
                pe.wait_ge(out_ready, at(n, 4, j, 4))
                for p in range(PAIRS):
                    mm = pe.matmul(OT[:, 0:P], wo[:, p * D:(p + 1) * D], outT[:, p, :],
                                   start=(p == 0), stop=(p == PAIRS - 1))
                mm.then_inc(y_full, 1)

            def sequence(s, n, last):
                for now, value, todo, nxt, turn, y in schedule(last):
                    if now:
                        scores(n, now[0], 2 * now[1])
                        scores(n, now[0], 2 * now[1] + 1)
                    if value:
                        values(n, *value)
                    pieces(n, nxt, todo, s)
                    if turn:
                        turn_probs(n, *turn)
                    if y is not None:
                        output(n, y)

            def feed_forward(L):
                n = L * SEQS

                def mean(s):
                    pe.wait_ge(shifted_ffn, n + s + 1)
                    if s == 0:
                        pe.wait_ge(rotated, at(n + SEQS, 4, -1, 4))
                    if s >= 2:
                        pe.wait_ge(z_ffn, n + s - 1 + 1)
                    pe.matmul(PJ[0][:, :], M.mean_w[:, :], xs[:, s * T:(s + 1) * T],
                              start=True, stop=True).then_inc(mean_full, 1)

                def variance(s):
                    pe.wait_ge(sqf_ready, n + s + 1)
                    if s > 0:
                        pe.wait_ge(xn_scaled, n + s)
                    for i in range(TILES):
                        mm = pe.matmul(PJ[1][:, i:i + 1], sq[:, s % 2, i * P:(i + 1) * P], M.mean_w[:, 0:1],
                                       start=True, stop=True)
                    mm.then_inc(var_full, 1)

                def spread(s):
                    pe.wait_ge(rstd_step, (n + s) * NEWTON + NEWTON)
                    for i in range(TILES):
                        mm = pe.matmul(PJ[1][:, i * P:(i + 1) * P], rstd[:, s % 2, i:i + 1].broadcast_to([P, P]),
                                       M.ident[:, :], start=True, stop=True)
                    mm.then_inc(rstd_full, 1)

                def first(s, base, banks, used, full):
                    for k in range(FBLK):
                        pe.wait_ge(used, n * FBLK + (s * FBLK + k + 1))
                        pe.matmul(banks[k][0:blk(k), :], w1[:, base + k * P:base + k * P + blk(k)], xn[:, s % 2, :],
                                  start=True, stop=True).then_inc(full, 1)
                mean(0)
                pe.wait_ge(v_ready, at(n + SEQS, 2, -1, 2))
                variance(0)
                spread(0)
                pe.wait_ge(turned_ready, at(n + SEQS, 4, -1, 4))
                pe.wait_ge(exp_done, at(n + SEQS, 8, -1, 8))
                pe.wait_ge(pt_ready, at(n + SEQS, 4, -1, 4))
                pe.wait_ge(z_attn, at(n + SEQS, 1, -1, 1))
                for s in range(SEQS):
                    if s + 1 < SEQS:
                        mean(s + 1)
                    pe.wait_ge(xn_ready, n + s + 1)
                    first(s, FF, [SC[0], SC[1], TQ], gelu_done, gate_full)
                    if s + 1 < SEQS:
                        variance(s + 1)
                    first(s, 0, [PTB, PX, OT], hid_ready, lin_full)
                    if s + 1 < SEQS:
                        spread(s + 1)
                        pe.wait_ge(centred, n + s + 2)
                    for k in range(FBLK):
                        pe.wait_ge(hid_ready, n * FBLK + (s * FBLK + k + 1 + FBLK))
                        mm = pe.matmul(PJ[0][:, :], w2[0:blk(k), k * D:(k + 1) * D], hid[0:blk(k), k, :],
                                       start=(k == 0), stop=(k == FBLK - 1))
                    mm.then_inc(ffn_full, 1)

            pe.wait_ge(cleared, 5)
            with pe.Fori(0, DEPTH) as L:
                pe.wait_ge(qkv_loaded, L * 32 + 32)
                pe.wait_ge(xa_first, L * SEQS + 1)
                pe.wait_ge(z_ffn, L * SEQS + 1)
                pieces(L * SEQS, 0, PROLOGUE, 0)
                pe.wait_ge(rest_loaded, L * 64 + 64)
                pe.sem_inc(pe_passed, 1)
                with pe.Fori(0, SEQS - 1) as s:
                    n = L * SEQS + s
                    sequence(s, n, False)
                sequence(SEQS - 1, L * SEQS + (SEQS - 1), True)
                feed_forward(L)

        @block.scalar
        def _(act):
            sem_start(act, [(squared, 4), (v_ready, 2), (turned_ready, 4), (exp_done, 8), (out_ready, 4)])
            act.sem_inc(gelu_done, FBLK)

            def pieces(n, j, todo):
                for what in todo:
                    if what[0] == "T":
                        name_, grp = what[1], int(what[2])
                        act.wait_ge(turned_full, at(n, 4, j, ROT.index(what[1:]) + 1))
                        src = TQ[:, :].rearrange("p (c t) -> p c t", t=P)
                        if name_ == "q":
                            act.activation(qT[0:64, j % 2, 4 * grp:4 * grp + 4, 0, :], src[0:64], ACT.Copy)
                            act.activation(qT[64:P, j % 2, 4 * grp:4 * grp + 4, 1, :], src[64:P],
                                           ACT.Copy).then_inc(turned_ready, 1)
                        else:
                            c0 = WINDOW + (j % TILES) * P
                            act.activation(kT[:, 4 * grp:4 * grp + 4, c0:c0 + P], src, ACT.Copy).then_inc(turned_ready, 1)
                        continue
                    idx = PROJ.index(what)
                    act.wait_ge(proj_full, at(n, 6, j, idx + 1))
                    if what[0] == "v":
                        if what == "v0":
                            act.wait_ge(out_full, at(n, 4, j - 2, 4))
                            if j >= 2:
                                act.wait_ge(prev_loaded[(j - 1) % 2], prev_count(n, j - 1))
                        g = int(what[1])
                        act.activation(V[:, j % 2, g * T:(g + 1) * T], PJ[idx % 2][:, :], ACT.Copy).then_inc(v_ready, 1)
                    else:
                        f = ROT.index(what)
                        act.wait_ge(rotated, at(n, 4, j, f - 1))
                        act.activation(sq[:, f % 2, :], PJ[idx % 2][:, :], ACT.Square).then_inc(squared, 1)

            def exponentials(n, j, g):
                act.wait_ge(pt_full, at(n, 4, j, g - 1))
                for p in (2 * g, 2 * g + 1):
                    act.wait_ge(max_ready, at(n, 8, j, p + 1))
                    act.wait_ge(recip_ready, at(n, 8, j, p - 3))
                    for c in range(2):
                        last = act.activation(prob[:, g % 2, 2 * (p % 2) + c, :], SC[p % 2][:, c * KEYS:(c + 1) * KEYS],
                                              ACT.Exp, bias=negmax[:, p % 4, c:c + 1],
                                              accum_out=total[:, p % 4, c:c + 1])
                    last.then_inc(exp_done, 1)

            def sequence(s, n, last):
                for now, value, todo, nxt, turn, y in schedule(last):
                    if now:
                        exponentials(n, *now)
                    if value:
                        j, g = value
                        act.wait_ge(out_full, at(n, 4, j, g + 1))
                        if g == 0:
                            act.wait_ge(y_full, at(n, 1, j - 1, 1))
                        act.activation(outT[:, 2 * g:2 * g + 2, :], OT[:, 0:2 * P].rearrange("p (c t) -> p c t", t=P),
                                       ACT.Copy).then_inc(out_ready, 1)
                    pieces(n, nxt, todo)

            def feed_forward(L):
                n = L * SEQS

                def square(s):
                    act.wait_ge(centred, n + s + 1)
                    if s >= 2:
                        act.wait_ge(var_full, n + s - 1)
                    act.activation(sq[:, s % 2, :], xc[:, s % 2, :], ACT.Square).then_inc(sqf_ready, 1)

                square(0)
                for s in range(SEQS):
                    if s + 1 < SEQS:
                        square(s + 1)
                    for k in range(FBLK):
                        act.wait_ge(gate_full, n * FBLK + (s * FBLK + k + 1))
                        act.wait_ge(hid_ready, n * FBLK + (s * FBLK + k + 1))
                        act.activation(gg[0:blk(k), k, :], [SC[0], SC[1], TQ][k][0:blk(k), :], ACT.Gelu,
                                       bias=vec[0:blk(k), FBLK + k:FBLK + k + 1]).then_inc(gelu_done, 1)

            with act.Fori(0, DEPTH) as L:
                pieces(L * SEQS, 0, PROLOGUE)
                sequences(act, L, sequence)
                act.wait_ge(rest_loaded, L * 64 + 64)
                feed_forward(L)

        @block.gpsimd
        def _(pool):
            sem_start(pool, [(qk_ready, 4), (prob_ready, 8), (proj_full, 6), (turned_full, 4), (score_full, 8),
                             (pt_full, 4), (out_full, 4), (y_full, 1)])
            pool.memset(Vp[:, :, :, :], 0.0).then_inc(cleared, 1)
            pool.memset(kT[:, :, :], 0.0).then_inc(cleared, 1)
            pool.memset(qT[:, :, :, :, :], 0.0).then_inc(cleared, 1)
            pool.memset(xs[:, :], 0.0).then_inc(cleared, 1)
            pool.memset(xa[:, :], 0.0).then_inc(cleared, 1)

            def add(n, j, what):
                f = ROT.index(what)
                pool.wait_ge(rotated, at(n, 4, j, f + 1))
                pool.tensor_tensor(rc[:, f % 2, :], rc[:, f % 2, :], rs[:, f % 2, :], ALU.add).then_inc(sum_ready, 1)
                pool.wait_ge(sum_ready, n * 16 + (j * 4 + f + 1))
                pool.wait_ge(norm_step, n * (16 * NEWTON) + (j * 4 + f + 1) * NEWTON)
                pool.wait_ge(turned_full, at(n, 4, j, f - 1))
                pool.tensor_tensor(qk[:, f % 2, :].rearrange("p (h d) -> p h d", d=DH),
                                   rc[:, f % 2, :].rearrange("p (h d) -> p h d", d=DH),
                                   rn[:, f % 2, :].rearrange("p (h o) -> p h o", o=1).broadcast_to([P, 8, DH]),
                                   ALU.mult).then_inc(qk_ready, 1)

            def normalise(n, j, p):
                pool.wait_ge(recip_ready, at(n, 8, j, p + 1))
                two = slice(2 * (p % 2), 2 * (p % 2) + 2)
                by = recip[:, p % 4, :].rearrange("p (h o) -> p h o", o=1)
                pool.tensor_tensor(prob_prev[:, (p // 2) % 2, two, :], prob[:, (p // 2) % 2, two, 0:WINDOW],
                                   by.broadcast_to([P, 2, WINDOW]), ALU.mult)
                v = prob[:, (p // 2) % 2, two, WINDOW:KEYS]
                pool.tensor_tensor(v, v, by.broadcast_to([P, 2, P]), ALU.mult).then_inc(prob_ready, 1)

            def sequence(s, n, last):
                for now, value, todo, nxt, turn, y in schedule(last):
                    rots = [w for w in todo if w in ROT]
                    for w in rots[:1]:
                        add(n, nxt, w)
                    if now:
                        normalise(n, now[0], 2 * now[1])
                        normalise(n, now[0], 2 * now[1] + 1)
                    for w in rots[1:]:
                        add(n, nxt, w)

            with pool.Fori(0, DEPTH) as L:
                for w in ROT:
                    add(L * SEQS, 0, w)
                sequences(pool, L, sequence)

        @block.vector
        def _(dve):
            sem_start(dve, [(rotated, 4), (max_ready, 8), (recip_ready, 8), (pt_ready, 4), (z_attn, 1)])
            dve.sem_inc(z_ffn, 1)
            dve.sem_inc(hid_ready, FBLK)
            dve.sem_inc(tables_ready, 1)
            dve.wait_ge(cleared, 5)

            def shift(s):
                dve.tensor_copy(xs[0:64, ds(s * T, T)], z[0:64, ds(s * T, T)])
                dve.tensor_copy(xs[64:P, ds(s * T + 1, T - 1)], z[64:P, ds(s * T, T - 1)]).then_inc(shifted_ffn, 1)

            def shift_first(s):
                dve.tensor_copy(xa[0:64, 0:P], z[0:64, ds(s * T, P)])
                dve.tensor_copy(xa[64:P, 1:P], z[64:P, ds(s * T, P - 1)]).then_inc(xa_first, 1)

            def shift_rest(s):
                dve.tensor_copy(xa[0:64, P:T], z[0:64, ds(s * T + P, T - P)])
                dve.tensor_copy(xa[64:P, P:T], z[64:P, ds(s * T + P - 1, T - P)]).then_inc(xa_rest, 1)

            shift_first(0)
            shift_rest(0)

            def rotate(n, j, what):
                f, idx = ROT.index(what), PROJ.index(what)
                c = 0 if what[0] == "q" else 2
                bank, tile = PJ[idx % 2], j % TILES
                dve.wait_ge(squared, at(n, 4, j, f + 1))
                dve.wait_ge(qk_ready, at(n, 4, j, f - 1))
                tab = lambda a, lo, n_: rot[:, a, tile, lo:lo + n_].rearrange("p (o d) -> p o d", o=1)
                dve.tensor_tensor(rc[:, f % 2, :].rearrange("p (h d) -> p h d", d=DH),
                                  bank[:, :].rearrange("p (h d) -> p h d", d=DH),
                                  tab(c, 0, DH).broadcast_to([P, 8, DH]), ALU.mult)
                for half in range(2):
                    dve.tensor_tensor(
                        rs[:, f % 2, :].rearrange("p (h a d) -> p h a d", a=2, d=DH // 2)[:, :, half, :],
                        bank[:, :].rearrange("p (h a d) -> p h a d", a=2, d=DH // 2)[:, :, 1 - half, :],
                        tab(c + 1, half * (DH // 2), DH // 2).broadcast_to([P, 8, DH // 2]), ALU.mult)
                dve.tensor_reduce(ssq[:, f % 2, :], sq[:, f % 2, :].rearrange("p (h d) -> p h d", d=DH),
                                  AX_X, ALU.add).then_inc(rotated, 1)
                dve.wait_ge(rotated, at(n, 4, j, f + 1))
                inverse_sqrt(dve, norm_step, n * (16 * NEWTON) + (j * 4 + f) * NEWTON, ssq[:, f % 2, :], ssq[:, f % 2, :],
                             rn[:, f % 2, :], rt[:, f % 2, :], ALU.max, 1e-24)

            def maximum(n, j, p):
                dve.wait_ge(score_full, at(n, 8, j, p + 1))
                dve.wait_ge(exp_done, at(n, 8, j, p - 3))
                dve.tensor_reduce(negmax[:, p % 4, :], SC[p % 2][:, 0:2 * KEYS].rearrange("p (h k) -> p h k", k=KEYS),
                                  AX_X, ALU.max, negate=True).then_inc(max_ready, 1)

            def reciprocal(n, j, p):
                dve.wait_ge(exp_done, at(n, 8, j, p + 1))
                dve.wait_ge(prob_ready, at(n, 8, j, p - 3))
                dve.reciprocal(recip[:, p % 4, :], total[:, p % 4, :]).then_inc(recip_ready, 1)

            def copy_probs(n, j, g):
                dve.wait_ge(pt_full, at(n, 4, j, g + 1))
                dve.wait_ge(out_full, at(n, 4, j, g - 1))
                dve.tensor_copy(PT[:, g % 2, :, :], PTB[:, :].rearrange("p (h t) -> p h t", t=P))
                dve.tensor_copy(PTp[:, g % 2, :], PX[:, 0:P]).then_inc(pt_ready, 1)

            def sequence(s, n, last):
                for now, value, todo, nxt, turn, y in schedule(last):
                    rots = [w for w in todo if w in ROT]
                    if now == (2, 0) and not last:
                        dve.wait_ge(proj_full, at(n, 6, 0, 6))
                        shift_first(s + 1)
                    if now == (3, 0) and not last:
                        dve.wait_ge(proj_full, at(n, 6, TILES - 1, 6))
                        shift_rest(s + 1)
                    if value:
                        copy_probs(n, *value)
                    if now:
                        maximum(n, now[0], 2 * now[1])
                        maximum(n, now[0], 2 * now[1] + 1)
                    for w in rots[:1]:
                        rotate(n, nxt, w)
                    if now:
                        reciprocal(n, now[0], 2 * now[1])
                        reciprocal(n, now[0], 2 * now[1] + 1)
                    for w in rots[1:]:
                        rotate(n, nxt, w)
                    if y is not None:
                        dve.wait_ge(y_full, at(n, 1, y, 1))
                        cols = ds(s * T + y * P, P)
                        dve.tensor_tensor(z[:, cols], z[:, cols], OT[:, 0:P], ALU.add).then_inc(z_attn, 1)
                dve.wait_ge(z_attn, at(n, 1, TILES - 1, 1))
                shift(s)

            def feed_forward(L):
                n = L * SEQS

                def centre(s):
                    dve.wait_ge(mean_full, n + s + 1)
                    dve.wait_ge(shifted_ffn, n + s + 1)
                    dve.tensor_tensor(xc[:, s % 2, :], xs[:, s * T:(s + 1) * T], PJ[0][:, :],
                                      ALU.subtract).then_inc(centred, 1)

                def deviation(s):
                    dve.wait_ge(var_full, n + s + 1)
                    inverse_sqrt(dve, rstd_step, (n + s) * NEWTON, PJ[1][:, 0:TILES], var[:, s % 2, :],
                                 rstd[:, s % 2, :], vt[:, s % 2, :], ALU.add, LN_EPS)

                def normal(s):
                    dve.wait_ge(rstd_full, n + s + 1)
                    if s >= 2:
                        dve.wait_ge(lin_full, n * FBLK + FBLK * (s - 1))
                    dve.tensor_tensor(xn[:, s % 2, :], xc[:, s % 2, :], PJ[1][:, :], ALU.mult).then_inc(xn_scaled, 1)
                    dve.wait_ge(xn_scaled, n + s + 1)
                    dve.tensor_scalar(xn[:, s % 2, :], xn[:, s % 2, :], vec[:, 2 * FBLK + 1:2 * FBLK + 2],
                                      vec[:, 2 * FBLK + 2:2 * FBLK + 3], ALU.mult, ALU.add).then_inc(xn_ready, 1)

                centre(0)
                deviation(0)
                dve.wait_ge(rest_loaded, L * 64 + 64)
                normal(0)
                for s in range(SEQS):
                    if s + 1 < SEQS:
                        centre(s + 1)
                        deviation(s + 1)
                    for k in range(FBLK):
                        dve.wait_ge(lin_full, n * FBLK + (s * FBLK + k + 1))
                        dve.wait_ge(gelu_done, n * FBLK + (s * FBLK + k + 1 + FBLK))
                        if k == 0:
                            dve.wait_ge(ffn_full, n + s + 1)
                        dve.scalar_tensor_tensor(out=hid[0:blk(k), k, :], in0=[PTB, PX, OT][k][0:blk(k), :],
                                                 scalar=vec[0:blk(k), k:k + 1], in1=gg[0:blk(k), k, :],
                                                 op0=ALU.add, op1=ALU.mult).then_inc(hid_ready, 1)
                    if s + 1 < SEQS:
                        normal(s + 1)
                    dve.wait_ge(ffn_full, n + s + 1 + 1)
                    dve.scalar_tensor_tensor(out=z[:, s * T:(s + 1) * T], in0=PJ[0][:, :],
                                             scalar=vec[:, 2 * FBLK:2 * FBLK + 1], in1=z[:, s * T:(s + 1) * T],
                                             op0=ALU.add, op1=ALU.add).then_inc(z_ffn, 1)
                    if s == 0:
                        dve.wait_ge(z_ffn, n + s + 2)
                        shift_first(0)
                        shift_rest(0)

            dve.sem_inc(ffn_full, 1)
            with dve.Fori(0, DEPTH) as L:
                dve.wait_ge(qkv_loaded, L * 32 + 32)
                for a in range(4):
                    dve.tensor_tensor(rot[:, a, :, :], M.tables[:, a, :, :],
                                      scales[:, a, :].rearrange("p (o d) -> p o d", o=1).broadcast_to([P, TILES, DH]),
                                      ALU.mult).then_inc(tables_ready, 1)
                dve.wait_ge(tables_ready, L * 4 + 5)
                for w in ROT:
                    rotate(L * SEQS, 0, w)
                sequences(dve, L, sequence)
                feed_forward(L)
            dve.wait_ge(z_ffn, DEPTH * SEQS + 1)
            dve.scalar_tensor_tensor(out=M.x[:, :], in0=z[:, :], scalar=0.5, in1=M.x[:, :],
                                     op0=ALU.mult, op1=ALU.add).then_inc(x_added, 1)


def full_attention_block(nc, M, W):
    UNITS = 4 * TILES
    LAST = UNITS + 3
    with ExitStack() as ctx:
        sem = stage_semaphores(nc, ctx, "full")
        sb = lambda n, s, d=F32: ctx.enter_context(nc.sbuf_tensor(f"full_{n}", s, d))
        proj_full, part_ready, rest_ready, v_ready, q_stacked, k_stacked = (
            sem(n) for n in ("proj_full", "part_ready", "rest_ready", "v_ready", "q_stacked", "k_stacked"))
        stack_full, stack_act, stack_dve, prepared = (
            sem(n) for n in ("stack_full", "stack_act", "stack_dve", "prepared"))
        score_full, max_ready, exp_done, recip_ready, coef_ready, weighted, mixed = (
            sem(n) for n in ("score_full", "max_ready", "exp_done", "recip_ready", "coef_ready", "weighted", "mixed"))
        pt_full, pt_ready, out_full, out_ready, y_full, x_updated, cleared = (
            sem(n) for n in ("pt_full", "pt_ready", "out_full", "out_ready", "y_full", "x_updated", "cleared"))
        coefs = sb("coefs", [P, 2])
        part = sb("part", [P, 2, SPLITS, 3 * D], BF16)
        rest = sb("rest", [P, 2, 2, 3 * D])
        stack = sb("stack", [P, TILES, 3, AH, STACK], BF16)
        QK = sb("QK", [STACK, 3, AH, T], BF16)
        V = sb("V", [P, TILES, AH, 32])
        negmax = sb("negmax", [P, 4, 2])
        total = sb("total", [P, 4, 2])
        recip = sb("recip", [P, 4, 2])
        weight = sb("weight", [P, 4, 2])
        prob = sb("prob", [P, 4, 2, T])
        PT = sb("PT", [P, 2, TILES, P])
        outT = sb("outT", [P, 2, T])
        xcur = sb("xcur", [P, T])
        Vg = sb("Vg", [P, TILES, P])
        wog = sb("wog", [P, D])
        xcur_ready, group_ready = sem("xcur_ready"), sem("group_ready")
        passed, pool_passed = sem("passed"), sem("pool_passed")
        block = ctx.enter_context(nc.Block())
        B = M.bank
        QK_flat = QK[:, :, :, :].rearrange("r y h t -> r (y h t)")

        def rows(s, g, u):
            return s * (4 * UNITS) + g * UNITS + u

        @block.tensor
        def _(pe):
            pe.wait_ge(M.full_loaded, 16 * M.full_dmas)
            pe.wait_ge(cleared, 3)
            with pe.Fori(0, SEQS) as s:
                for i in range(TILES):
                    if i == 0:
                        pe.wait_ge(exp_done, rows(s, 0, 2))
                        pe.wait_ge(xcur_ready, s + 1)
                    pe.matmul(B[i][:, :], xcur[:, i * P:(i + 1) * P], M.w4[:, :],
                              start=True, stop=True).then_inc(proj_full, 1)
                for c in range(3 * AH // 2):
                    if c == 0:
                        pe.wait_ge(q_stacked, s * TILES + TILES)
                        pe.wait_ge(k_stacked, s * TILES + TILES)
                        pe.wait_ge(pt_ready, rows(s, 0, 2))
                        pe.wait_ge(out_ready, s * 4 + 1)
                        pe.wait_ge(x_updated, s * 4 + 1)
                    if c >= 4:
                        pe.wait_ge([stack_act, stack_dve][c % 2], s * 12 + (c // 2 - 1))
                    bank16 = B[4 + c % 4][0:STACK, :].bitcast(BF16)
                    y, hp = c // (AH // 2), c % (AH // 2)
                    for hh in range(2):
                        for i in range(TILES):
                            mm = pe.transpose(bank16[:, hh * T + i * P:hh * T + (i + 1) * P],
                                              stack[:, i, y, 2 * hp + hh, :], M.ident16[:, :])
                    mm.then_inc(stack_full, 1)
                pe.wait_ge(stack_act, s * 12 + 12)
                pe.wait_ge(stack_dve, s * 12 + 12)
                pe.sem_inc(passed, 1)
                with pe.Fori(0, 4) as g:
                    for n in range(LAST):
                        if n < UNITS:
                            j, i = n // TILES, n % TILES
                            pe.wait_ge(exp_done, rows(s, g, n + 1))
                            for y in range(2):
                                mm = pe.matmul(B[2 * (n % 2) + y][:, :], QK_flat[:, ds(g * (4 * T) + (j * T + i * P), P)],
                                               QK_flat[:, ds(g * (4 * T) + ((1 + y) * AH * T + j * T), T)],
                                               start=True, stop=True)
                            mm.then_inc(score_full, 1)
                        if 2 <= n < UNITS + 2:
                            u = n - 2
                            pe.wait_ge(mixed, rows(s, g, u + 1))
                            pe.wait_ge(pt_ready, rows(s, g, u + 1))
                            for kb in range(TILES):
                                mm = pe.transpose(B[4 + u % 2][:, kb * P:(kb + 1) * P],
                                                  prob[:, u % 4, 0, kb * P:(kb + 1) * P], M.ident[:, :])
                            mm.then_inc(pt_full, 1)
                        if n >= 3:
                            u = n - 3
                            j, i = u // TILES, u % TILES
                            pe.wait_ge(pt_ready, rows(s, g, u + 1 + 2))
                            if u == 0:
                                pe.wait_ge(group_ready, s * 4 + g + 1)
                                pe.wait_ge(out_ready, s * 4 + g + 1)
                            for kb in range(TILES):
                                mm = pe.matmul(B[6][32 * j:32 * j + 32, i * P:(i + 1) * P],
                                               Vg[:, kb, 32 * j:32 * j + 32],
                                               PT[:, u % 2, kb, :], start=(kb == 0), stop=(kb == TILES - 1))
                            mm.then_inc(out_full, 1)
                    pe.wait_ge(out_ready, s * 4 + g + 2)
                    pe.wait_ge(x_updated, s * 4 + g + 1)
                    pe.matmul(B[7][:, :], wog[:, :], outT[:, 0, :], start=True, stop=True).then_inc(y_full, 1)

        @block.scalar
        def _(act):
            act.sem_inc(exp_done, 2)
            act.sem_inc(out_ready, 1)
            with act.Fori(0, SEQS) as s:
                for i in range(TILES):
                    act.wait_ge(proj_full, s * TILES + (i + 2))
                    b = i % 2
                    if i >= 2:
                        act.wait_ge(q_stacked, s * TILES + (i - 1))
                        act.wait_ge(k_stacked, s * TILES + (i - 1))
                    act.activation(V[:, i, :, 0:AD], B[i][:, 3 * D:4 * D].rearrange("p (h d) -> p h d", d=AD),
                                   ACT.Copy).then_inc(v_ready, 1)
                    act.activation(part[:, b, 0, :], B[i][:, 0:3 * D], ACT.Copy).then_inc(part_ready, 1)
                    for a in range(1, SPLITS):
                        act.wait_ge(rest_ready, s * (2 * TILES) + (2 * i + a))
                        act.activation(part[:, b, a, :], rest[:, b, a - 1, :], ACT.Copy).then_inc(part_ready, 1)
                for c in range(0, 3 * AH // 2, 2):
                    act.wait_ge(stack_full, s * 24 + (c + 2))
                    act.activation(QK_flat[:, c * 2 * T:(c + 1) * 2 * T], B[4 + c % 4][0:STACK, :].bitcast(BF16),
                                   ACT.Copy).then_inc(stack_act, 1)
                with act.Fori(0, 4) as g:
                    for n in range(LAST):
                        if n < UNITS:
                            act.wait_ge(max_ready, rows(s, g, n + 1))
                            act.wait_ge(pt_full, rows(s, g, n + 1))
                            for y in range(2):
                                last = act.activation(prob[:, n % 4, y, :], B[2 * (n % 2) + y][:, :], ACT.Exp,
                                                      bias=negmax[:, n % 4, y:y + 1], accum_out=total[:, n % 4, y:y + 1])
                            last.then_inc(exp_done, 1)
                        if n >= 3:
                            u = n - 3
                            act.wait_ge(pt_full, rows(s, g, u + 1 + 4))
                            act.wait_ge(out_full, rows(s, g, u + 1))
                            act.activation(PT[:, u % 2, :, :], B[4 + u % 2][:, :].rearrange("p (k t) -> p k t", t=P),
                                           ACT.Copy).then_inc(pt_ready, 1)
                    act.wait_ge(out_full, rows(s, g, UNITS + 2))
                    act.wait_ge(y_full, s * 4 + g + 1)
                    act.activation(outT[:, 0, :], B[6][:, :], ACT.Copy).then_inc(out_ready, 1)

        @block.gpsimd
        def _(pool):
            pool.sem_inc(pt_ready, 2)
            pool.sem_inc(pt_full, 4)
            pool.sem_inc(out_full, 2)
            pool.sem_inc(y_full, 1)
            pool.memset(V[:, :, :, :], 0.0).then_inc(cleared, 1)
            V_flat = V[:, :, :, :].rearrange("p k h d -> p k (h d)")
            with pool.Fori(0, SEQS) as s:
                for i in range(TILES):
                    for a in range(SPLITS):
                        pool.wait_ge(part_ready, s * (SPLITS * TILES) + (SPLITS * i + a + 1))
                        pool.sem_inc(pool_passed, 1)
                        last = pool.tensor_copy(
                            stack[:, i, 0, :, :].rearrange("p h (a b d) -> p h a b d", a=SPLITS, d=AD)[:, :, a, :, :],
                            part[:, i % 2, a, 0:D].rearrange("p (h o d) -> p h o d", o=1, d=AD)
                            .broadcast_to([P, AH, SPLITS, AD]))
                    last.then_inc(q_stacked, 1)
                with pool.Fori(0, 4) as g:
                    pool.wait_ge(v_ready, s * TILES + TILES)
                    pool.wait_ge(y_full, s * 4 + g + 1)
                    pool.sem_inc(pool_passed, 1)
                    pool.tensor_copy(Vg[:, :, :], V_flat[:, :, ds(g * P, P)])
                    pool.tensor_copy(wog[:, :], M.wo_full[:, ds(g * D, D)]).then_inc(group_ready, 1)
                    for n in range(UNITS):
                        pool.wait_ge(coef_ready, rows(s, g, n + 1))
                        pool.tensor_tensor(prob[:, n % 4, 0, :], prob[:, n % 4, 0, :],
                                           weight[:, n % 4, 0:1].broadcast_to([P, T]), ALU.mult).then_inc(weighted, 1)

        @block.vector
        def _(dve):
            dve.sem_inc(x_updated, 1)
            dve.sem_inc(proj_full, 1)
            dve.sem_inc(stack_full, 1)
            dve.wait_ge(M.full_loaded, 16 * M.full_dmas)
            dve.tensor_scalar(coefs[:, 1:2], M.alpha[:, :], -1.0, 1.0, ALU.mult, ALU.add)
            dve.tensor_copy(coefs[:, 0:1], M.alpha[:, :]).then_inc(cleared, 1)
            dve.tensor_scalar(M.w4[:, 0:D], M.w4[:, 0:D], AD ** -0.5, None, ALU.mult).then_inc(cleared, 1)
            dve.wait_ge(cleared, 3)
            with dve.Fori(0, SEQS) as s:
                dve.wait_ge(proj_full, s * TILES + 1)
                dve.tensor_copy(xcur[:, :], M.xh[:, ds(s * T, T)]).then_inc(xcur_ready, 1)
                for i in range(TILES):
                    b = i % 2
                    dve.wait_ge(part_ready, s * (SPLITS * TILES) + (SPLITS * i + 1))
                    if i == 0:
                        dve.wait_ge(stack_full, s * 24 + 1)
                    dve.tensor_tensor(rest[:, b, 0, :], B[i][:, 0:3 * D], part[:, b, 0, :], ALU.subtract).then_inc(rest_ready, 1)
                    dve.wait_ge(part_ready, s * (SPLITS * TILES) + (SPLITS * i + 2))
                    dve.wait_ge(rest_ready, s * (2 * TILES) + (2 * i + 1))
                    dve.tensor_tensor(rest[:, b, 1, :], rest[:, b, 0, :], part[:, b, 1, :], ALU.subtract).then_inc(rest_ready, 1)
                    dve.wait_ge(part_ready, s * (SPLITS * TILES) + (SPLITS * i + 3))
                    for a in range(SPLITS):
                        last = dve.tensor_copy(
                            stack[:, i, 1:3, :, :].rearrange("p y h (b a d) -> p (y h) b a d", a=SPLITS, d=AD)[:, :, :, a, :],
                            part[:, b, a, D:3 * D].rearrange("p (h o d) -> p h o d", o=1, d=AD)
                            .broadcast_to([P, 2 * AH, SPLITS, AD]))
                    last.then_inc(k_stacked, 1)
                for c in range(1, 3 * AH // 2, 2):
                    dve.wait_ge(stack_full, s * 24 + (c + 2))
                    dve.tensor_copy(QK_flat[:, c * 2 * T:(c + 1) * 2 * T],
                                    B[4 + c % 4][0:STACK, :].bitcast(BF16)).then_inc(stack_dve, 1)
                with dve.Fori(0, 4) as g:
                    for n in range(LAST):
                        if n < UNITS:
                            dve.wait_ge(score_full, rows(s, g, n + 1))
                            dve.tensor_reduce(negmax[:, n % 4, :], M.psum[:, 2 * (n % 2):2 * (n % 2) + 2, :],
                                              AX_X, ALU.max, negate=True).then_inc(max_ready, 1)
                        if 1 <= n <= UNITS:
                            u = n - 1
                            dve.wait_ge(exp_done, rows(s, g, u + 1 + 2))
                            dve.reciprocal(recip[:, u % 4, :], total[:, u % 4, :]).then_inc(recip_ready, 1)
                            dve.wait_ge(recip_ready, rows(s, g, u + 1))
                            dve.tensor_tensor(weight[:, u % 4, :], recip[:, u % 4, :], coefs[:, :], ALU.mult).then_inc(coef_ready, 1)
                        if 2 <= n < UNITS + 2:
                            u = n - 2
                            dve.wait_ge(weighted, rows(s, g, u + 1))
                            dve.scalar_tensor_tensor(out=prob[:, u % 4, 0, :], in0=prob[:, u % 4, 1, :],
                                                     scalar=weight[:, u % 4, 1:2], in1=prob[:, u % 4, 0, :],
                                                     op0=ALU.mult, op1=ALU.add).then_inc(mixed, 1)
                    dve.wait_ge(y_full, s * 4 + g + 2)
                    dve.tensor_tensor(M.x[:, ds(s * T, T)], M.x[:, ds(s * T, T)], B[7][:, :], ALU.add).then_inc(x_updated, 1)


def program(nc, A, out):
    M = Shared()
    with ExitStack() as ctx:
        sb = lambda n, s, d=F32: ctx.enter_context(nc.sbuf_tensor(n, s, d))
        sem = lambda n: ctx.enter_context(nc.semaphore(n))
        M.psum = ctx.enter_context(nc.psum_tensor("psum", [P, 8, 512], F32))
        M.bank = [M.psum[:, b, :] for b in range(8)]
        M.x = sb("x", [P, NTOK])
        M.xh = sb("xh", [P, NTOK])
        M.z = M.xh
        M.ident = sb("ident", [P, P])
        M.ident16 = sb("ident16", [P, P], BF16)
        M.mean_w = sb("mean_w", [P, P])
        M.tables = sb("tables", [P, 4, TILES, DH])
        mask32 = sb("mask32", [P, 2, 2 * KEYS])
        M.mask = sb("mask", [P, 2, 2 * KEYS], BF16)
        M.w4 = sb("w4", [P, 4 * D])
        M.wo_full = sb("wo_full", [P, 4 * D])
        M.alpha = sb("alpha", [P, 1])
        x_loaded, const_loaded, consts = sem("x_loaded"), sem("const_loaded"), sem("consts")
        M.moe_loaded, M.lin_loaded, M.full_loaded, stored = (
            sem("moe_loaded"), sem("lin_loaded"), sem("full_loaded"), sem("stored"))

        with ExitStack() as moe:
            sbm = lambda n, s, d=F32: moe.enter_context(nc.sbuf_tensor(n, s, d))
            M.wg = sbm("wg", [P, EXPERTS])
            M.bg = sbm("bg", [P, EXPERTS])
            M.b1 = sbm("moe_b1", [P, EXPERTS * HBLK])
            M.b2 = sbm("moe_b2", [EXPERTS, D])
            M.wq, M.wk, M.wv, M.wo_lin = (sbm(n, [P, LIN_HEADS // 2 * D]) for n in ("lin_wq", "lin_wk", "lin_wv", "lin_wo"))
            moe_loads = [(M.wg, "wg"), (M.b1, "moe_b1"), (M.b2, "moe_b2")]
            M.moe_dmas = len(moe_loads) + 1
            M.lin_dmas = 4
            M.full_dmas = 3
            with nc.Block() as block:
                @block.sync
                def _(sp):
                    for s in range(SEQS):
                        sp.dma_start(M.x[:, s * T:(s + 1) * T], A["xT"][:, s * T:(s + 1) * T]).then_inc(x_loaded, 16)
                    sp.dma_start(M.ident[:, :], A["ident"]).then_inc(const_loaded, 16)
                    sp.dma_start(mask32[:, :, :], A["mask"].rearrange("p (a k) -> p a k", a=2)).then_inc(const_loaded, 16)
                    sp.dma_start(M.tables[:, :, :, :], A["tables"].rearrange("p (a i d) -> p a i d", a=4, d=DH)).then_inc(const_loaded, 16)
                    for t, n in moe_loads:
                        sp.dma_start(t[:, :], A[n]).then_inc(M.moe_loaded, 16)
                    sp.dma_start(M.bg[:, :], A["bg"].broadcast_to([P, EXPERTS])).then_inc(M.moe_loaded, 16)
                    for t, n in ((M.wq, "lin_wq"), (M.wk, "lin_wk"), (M.wv, "lin_wv"), (M.wo_lin, "lin_wo")):
                        sp.dma_start(t[:, :], A[n]).then_inc(M.lin_loaded, 16)
                    sp.dma_start(M.w4[:, :], A["w4"]).then_inc(M.full_loaded, 16)
                    sp.dma_start(M.wo_full[:, :], A["wo_full"]).then_inc(M.full_loaded, 16)
                    sp.dma_start(M.alpha[:, :], A["alpha"].broadcast_to([P, 1])).then_inc(M.full_loaded, 16)
                    sp.wait_ge(x_loaded, 16 * SEQS)

                @block.vector
                def _(dve):
                    dve.memset(M.mean_w[:, :], 1.0 / D).then_inc(consts, 1)
                    dve.wait_ge(const_loaded, 48)
                    dve.tensor_copy(M.ident16[:, :], M.ident[:, :]).then_inc(consts, 1)
                    dve.tensor_copy(M.mask[:, :, :], mask32[:, :, :]).then_inc(consts, 1)

            layernorm_block(nc, M, M.x, M.xh, "ln0")
            expert_block(nc, M, A, "moe0")
            layernorm_block(nc, M, M.x, M.xh, "ln1")
            linear_attention_block(nc, M)
            layernorm_block(nc, M, M.x, M.xh, "ln2")
            expert_block(nc, M, A, "moe1")
        layernorm_block(nc, M, M.x, M.xh, "ln3")
        local_transformer_block(nc, M, A, "loc0")
        layernorm_block(nc, M, M.x, M.xh, "ln4")
        full_attention_block(nc, M, A)
        layernorm_block(nc, M, M.x, M.xh, "ln5")
        local_transformer_block(nc, M, A, "loc1")
        with nc.Block() as block:
            @block.sync
            def _(sp):
                sp.dma_start(out, M.x[:, :]).then_inc(stored, 16)
                for loaded, n in ((M.moe_loaded, M.moe_dmas), (M.lin_loaded, M.lin_dmas), (M.full_loaded, M.full_dmas)):
                    sp.wait_ge(loaded, 16 * n)
                sp.wait_ge(stored, 16)


def rotary_constants():
    f = np.float32
    half = np.arange(0, DH, 2).astype(f)
    inv_freq = f(1.0) / np.power(f(10000.0), half / f(DH)).astype(f)
    t = np.arange(T).astype(f)
    freqs = (t[:, None] * inv_freq[None, :]).astype(f)
    base = (half + f(0.4 * DH)) / f(1.4 * DH)
    power = (t - f(T // 2)) / f(WINDOW // 2)
    scale = np.power(base[None, :], power[:, None]).astype(f)
    cos, sin = np.cos(freqs.astype(np.float64)), np.sin(freqs.astype(np.float64))
    sc = scale.astype(np.float64)
    twice = lambda a, b: np.concatenate([a, b], -1)
    tabs = [twice(cos * sc, cos * sc) * QK_SCALE, twice(-sin * sc, sin * sc) * QK_SCALE,
            twice(cos / sc, cos / sc), twice(-sin / sc, sin / sc)]
    tab = np.stack(tabs).astype(f)
    return np.ascontiguousarray(tab.reshape(4, TILES, P, DH).transpose(2, 0, 1, 3).reshape(P, -1))


def mask_constant():
    q = np.arange(P)[:, None]
    c = np.arange(KEYS)[None, :]
    seen = (q <= c) & (c <= q + WINDOW)
    later = np.where(seen, 0.0, MASKED)
    firsts = np.where(seen & (c >= WINDOW), 0.0, MASKED)
    return np.concatenate([firsts, firsts, later, later], 1).astype(np.float32)


def layout(I):
    c = np.ascontiguousarray
    I = {k: np.asarray(v) for k, v in I.items()}
    pairs = lambda w: c(w.reshape(LIN_HEADS // 2, P, D).transpose(1, 0, 2).reshape(P, -1))
    L1 = "L1_ffn_"
    b1, vecs = I[L1 + "b1"], np.zeros((DEPTH, P, 2 * FBLK + 3), np.float32)
    w2 = np.zeros((DEPTH, P, FBLK, D), np.float32)
    for k in range(FBLK):
        n = blk(k)
        vecs[:, :n, k] = b1[:, k * P:k * P + n]
        vecs[:, :n, FBLK + k] = b1[:, FF + k * P:FF + k * P + n]
        w2[:, :n, k] = I[L1 + "W2"][:, k * P:k * P + n]
    for j, n in enumerate(("b2", "ln_g", "ln_b")):
        vecs[:, :, 2 * FBLK + j] = I[L1 + n]
    qs, ks = I[L1 + "q_scale"], I[L1 + "k_scale"]
    swap = lambda a: np.concatenate([a[:, DH // 2:], a[:, :DH // 2]], 1)
    wo_full = np.zeros((4, 4, 32, D), np.float32)
    wo_full[:, :, :AD] = I["L1_attn_W_O"].T.reshape(4, 4, AD, D)
    return {
        "xT": c(I["L0_attn_x"].reshape(NTOK, D).T),
        "ident": np.eye(P, dtype=np.float32), "mask": mask_constant(), "tables": rotary_constants(),
        "wg": I["L0_ffn_Wg"], "bg": I["L0_ffn_bg"].reshape(1, EXPERTS),
        "moe_w1": c(I["L0_ffn_W1"].transpose(1, 0, 2).reshape(D, -1)),
        "moe_w2": c(I["L0_ffn_W2"].reshape(EXPERTS, HBLK, P, D).transpose(2, 0, 1, 3).reshape(P, -1)),
        "moe_b1": c(I["L0_ffn_b1"].reshape(EXPERTS * HBLK, P).T), "moe_b2": I["L0_ffn_b2"],
        "lin_wq": pairs(I["L0_attn_W_q"]), "lin_wk": pairs(I["L0_attn_W_k"]), "lin_wv": pairs(I["L0_attn_W_v"]),
        "lin_wo": pairs(c(I["L0_attn_W_o"].T)),
        "w4": c(np.concatenate([I["L1_attn_" + n].T for n in ("W_Q", "W_K", "W_K_prime", "W_V")], 1)),
        "wo_full": c(wo_full.transpose(1, 2, 0, 3).reshape(P, -1)),
        "alpha": I["L1_attn_alpha"].reshape(1, 1),
        "wqkv": I[L1 + "Wqkv"], "w1": I[L1 + "W1"], "w2": c(w2.reshape(DEPTH, P, -1)), "vec": vecs,
        "wo": c(I[L1 + "Wo"].reshape(DEPTH, PAIRS, P, D).transpose(0, 2, 1, 3).reshape(DEPTH, P, -1)),
        "scales": c(np.concatenate([qs, swap(qs), ks, swap(ks)], 1)),
    }


def kernel(**I):
    import concourse.bacc as bacc
    from concourse.bass_utils import run_bass_kernel_spmd

    c = np.ascontiguousarray
    arrays = layout(I)
    nc = bacc.Bacc("TRN2", target_bir_lowering=False, num_devices=1)
    A = {n: nc.dram_tensor("in_" + n, a.shape, mybir.dt.from_np(a.dtype), kind="ExternalInput").ap() for n, a in arrays.items()}
    out = nc.dram_tensor("out_xT", (D, NTOK), F32, kind="ExternalOutput").ap()
    program(nc, A, out)
    r = run_bass_kernel_spmd(nc, [{"in_" + n: c(a) for n, a in arrays.items()}], core_ids=[0])
    return c(r.results[0]["out_xT"].T).reshape(SEQS, T, D)
```

```python
from contextlib import ExitStack

import numpy as np

import concourse.bass as bass
from concourse import mybir

ALU = mybir.AluOpType
ACT = mybir.ActivationFunctionType
AX_X = mybir.AxisListType.X
F32 = mybir.dt.float32
BF16 = mybir.dt.bfloat16

P = 128
D = 128
SEQS, T = 4, 512
TILES = T // P
NTOK = SEQS * T
LN_EPS = 1e-5
EXPERTS, HID = 8, 512
HBLK = HID // P
LIN_HEADS, LIN_DK = 16, 64
DEPTH, HEADS, DH, WINDOW = 6, 16, 64, 32
INNER = HEADS * DH
PAIRS = HEADS // 2
GROUPS = HEADS // 4
KEYS = P + WINDOW
FF = int(D * 4 * 2 / 3)
FBLK = -(-FF // P)
QK_SCALE = 8.0
MASKED = -1.0e30
AH, AD = 16, 8
SPLITS = 3
STACK = SPLITS * SPLITS * AD
CREDIT = 2
ds = bass.ds


def blk(k):
    return min(P, FF - k * P)


class Shared:
    pass


def sem_start(eng, sems):
    for s, per_tile in sems:
        eng.sem_inc(s, CREDIT * per_tile + 1)


LOW_BITS = -4096
F32R, I32 = mybir.dt.float32r, mybir.dt.int32
NEWTON = 11


def inverse_sqrt(dve, step, done, src, x, y, t, op, guard):
    i32 = mybir.dt.int32
    dve.tensor_scalar(x, src, guard, None, op).then_inc(step, 1)
    dve.wait_ge(step, done + 1)
    dve.tensor_scalar(y.bitcast(i32), x.bitcast(i32), -0.5, float(0x5F3759DF), ALU.mult, ALU.add).then_inc(step, 1)
    for k in range(3):
        dve.wait_ge(step, done + (3 * k + 2))
        dve.tensor_tensor(t, y, y, ALU.mult).then_inc(step, 1)
        dve.wait_ge(step, done + (3 * k + 3))
        dve.scalar_tensor_tensor(out=t, in0=t, scalar=-0.5, in1=x, op0=ALU.mult, op1=ALU.mult).then_inc(step, 1)
        dve.wait_ge(step, done + (3 * k + 4))
        dve.scalar_tensor_tensor(out=y, in0=t, scalar=1.5, in1=y, op0=ALU.add, op1=ALU.mult).then_inc(step, 1)


def stage_semaphores(nc, ctx, stage):
    used = []
    ctx.callback(nc.all_engine_barrier)
    ctx.callback(nc.clear_and_free_semaphores, used)

    def sem(name):
        used.append(nc.alloc_semaphore(f"{stage}_{name}"))
        return used[-1]
    return sem


def layernorm_block(nc, M, src, dst, name):
    with ExitStack() as ctx:
        sem = stage_semaphores(nc, ctx, name)
        sb = lambda n, s: ctx.enter_context(nc.sbuf_tensor(f"{name}_{n}", s, F32))
        mean_full, centred, squared, var_full, step, rstd_full, out_ready = (
            sem(n) for n in ("mean_full", "centred", "squared", "var_full", "step", "rstd_full", "out_ready"))
        sq = sb("sq", [P, 2, T])
        var, rstd, tmp = (sb(n, [P, SEQS, TILES]) for n in ("var", "rstd", "tmp"))
        block = ctx.enter_context(nc.Block())
        MEAN, VAR, RSTD = M.bank[0:2], M.bank[2:4], M.bank[4:6]

        @block.tensor
        def _(pe):
            def spread(s):
                pe.wait_ge(step, NEWTON * (s + 1))
                if s >= 2:
                    pe.wait_ge(out_ready, s - 1)
                for i in range(TILES):
                    mm = pe.matmul(RSTD[s % 2][:, i * P:(i + 1) * P], rstd[:, s, i:i + 1].broadcast_to([P, P]),
                                   M.ident[:, :], start=True, stop=True)
                mm.then_inc(rstd_full, 1)

            for s in range(SEQS):
                if s >= 2:
                    pe.wait_ge(centred, s - 1)
                pe.matmul(MEAN[s % 2][:, :], M.mean_w[:, :], src[:, s * T:(s + 1) * T],
                          start=True, stop=True).then_inc(mean_full, 1)
            for s in range(SEQS):
                pe.wait_ge(squared, s + 1)
                if s >= 2:
                    pe.wait_ge(step, NEWTON * (s - 1))
                for i in range(TILES):
                    mm = pe.matmul(VAR[s % 2][:, i:i + 1], sq[:, s % 2, i * P:(i + 1) * P], M.mean_w[:, 0:1],
                                   start=True, stop=True)
                mm.then_inc(var_full, 1)
                if s >= 1:
                    spread(s - 1)
            spread(SEQS - 1)

        @block.scalar
        def _(act):
            for s in range(SEQS):
                act.wait_ge(centred, s + 1)
                if s >= 2:
                    act.wait_ge(var_full, s - 1)
                act.activation(sq[:, s % 2, :], dst[:, s * T:(s + 1) * T], ACT.Square).then_inc(squared, 1)

        @block.vector
        def _(dve):
            def scale(s):
                dve.wait_ge(rstd_full, s + 1)
                dve.tensor_tensor(dst[:, s * T:(s + 1) * T], dst[:, s * T:(s + 1) * T], RSTD[s % 2][:, :],
                                  ALU.mult).then_inc(out_ready, 1)

            for s in range(SEQS):
                dve.wait_ge(mean_full, s + 1)
                dve.tensor_tensor(dst[:, s * T:(s + 1) * T], src[:, s * T:(s + 1) * T], MEAN[s % 2][:, :],
                                  ALU.subtract).then_inc(centred, 1)
            for s in range(SEQS):
                dve.wait_ge(var_full, s + 1)
                inverse_sqrt(dve, step, NEWTON * s, VAR[s % 2][:, 0:TILES], var[:, s, :], rstd[:, s, :], tmp[:, s, :],
                             ALU.add, LN_EPS)
                if s >= 1:
                    scale(s - 1)
            scale(SEQS - 1)


def expert_block(nc, M, W, name):
    UNITS = 2 * SEQS
    with ExitStack() as ctx:
        sem = stage_semaphores(nc, ctx, name)
        sb = lambda n, s, d=F32: ctx.enter_context(nc.sbuf_tensor(f"{name}_{n}", s, d))
        logits_full, logits_ready, prob_ready, gate_ready, gate_t_full, gate_t_ready = (
            sem(n) for n in ("logits_full", "logits_ready", "prob_ready", "gate_ready", "gate_t_full", "gate_t_ready"))
        passed = sem("passed")
        hid_full, relu_dve, relu_act, out_full, combined = (
            sem(n) for n in ("hid_full", "relu_dve", "relu_act", "out_full", "combined"))
        bias_full, bias_copied, back_full, x_updated = (
            sem(n) for n in ("bias_full", "bias_copied", "back_full", "x_updated"))
        loaded = [sem("loaded0"), sem("loaded1")]
        w1 = sb("w1", [P, 2, HID])
        w2 = sb("w2", [P, 2, HBLK, D])
        logit, prob, gate = (sb(n, [P, NTOK // P, EXPERTS]) for n in ("logit", "prob", "gate"))
        gate_t = sb("gate_t", [EXPERTS, NTOK])
        hid = sb("hid", [P, 2, HBLK, T])
        acc = sb("acc", [P, NTOK // P, D])
        block = ctx.enter_context(nc.Block())
        HB, YB, GB = M.bank[0:4], M.bank[4:6], M.bank[6:8]
        gate_cols = gate[:, :, :].rearrange("p t e -> p (t e)")

        @block.sync
        def _(sp):
            with sp.Fori(0, EXPERTS // 2) as e2:
                for u in range(2):
                    sp.wait_ge(out_full, e2 * UNITS + (u * SEQS + 2 - (SEQS if u else 0)))
                    sp.dma_start(w1[:, u, :], W["moe_w1"][:, ds(e2 * (2 * HID) + u * HID, HID)]).then_inc(loaded[u], 16)
                    sp.dma_start(w2[:, u, :, :], W["moe_w2"][:, ds(e2 * (2 * HBLK * D) + u * HBLK * D, HBLK * D)]
                                 .rearrange("p (k d) -> p k d", d=D)).then_inc(loaded[u], 16)

        @block.tensor
        def _(pe):
            pe.wait_ge(M.moe_loaded, 16 * M.moe_dmas)
            for t in range(NTOK // P):
                mm = pe.matmul(GB[0][:, t * EXPERTS:(t + 1) * EXPERTS], M.xh[:, t * P:(t + 1) * P], M.wg[:, :],
                               start=True, stop=True)
            mm.then_inc(logits_full, 1)
            pe.wait_ge(gate_ready, 1)
            for s in range(SEQS):
                for i in range(TILES):
                    mm = pe.transpose(HB[s][0:EXPERTS, i * P:(i + 1) * P], gate[:, s * TILES + i, :], M.ident[:, :])
                mm.then_inc(gate_t_full, 1)
            for s in range(SEQS):
                pe.wait_ge(gate_t_ready, s + 1)
                if s >= 2:
                    pe.wait_ge(bias_copied, s - 1)
                for i in range(TILES):
                    mm = pe.matmul(GB[s % 2][:, i * D:(i + 1) * D], gate_t[:, s * T + i * P:s * T + (i + 1) * P], M.b2[:, :],
                                   start=True, stop=True)
                mm.then_inc(bias_full, 1)
            with pe.Fori(0, EXPERTS // 2) as e2:
                def first(u, v, h):
                    for k in range(HBLK):
                        n = 2 * (u * SEQS + v) + k // 2 + 1
                        pe.wait_ge(relu_act if k % 2 else relu_dve, e2 * (2 * UNITS) + n)
                        pe.matmul(HB[k][:, :], w1[:, u, k * P:(k + 1) * P], M.xh[:, v * T:(v + 1) * T],
                                  start=True, stop=True).then_inc(hid_full, 1)

                def second(u, v, h):
                    n = u * SEQS + v
                    pe.wait_ge(relu_dve, e2 * (2 * UNITS) + (2 * n + 4))
                    pe.wait_ge(relu_act, e2 * (2 * UNITS) + (2 * n + 4))
                    pe.wait_ge(combined, e2 * UNITS + (n + 1))
                    for i in range(TILES):
                        for k in range(HBLK):
                            mm = pe.matmul(YB[h][:, i * D:(i + 1) * D], hid[:, h, k, i * P:(i + 1) * P], w2[:, u, k, :],
                                           start=(k == 0), stop=(k == HBLK - 1))
                    mm.then_inc(out_full, 1)

                for u in range(2):
                    pe.wait_ge(loaded[u], e2 * 32 + 32)
                    for v in range(0, SEQS, 2):
                        first(u, v, 0)
                        first(u, v + 1, 1)
                        second(u, v, 0)
                        second(u, v + 1, 1)
            pe.wait_ge(combined, EXPERTS * SEQS + 2)
            for s in range(SEQS):
                for i in range(TILES):
                    mm = pe.transpose(HB[s][:, i * P:(i + 1) * P], acc[:, s * TILES + i, :], M.ident[:, :])
                mm.then_inc(back_full, 1)

        @block.scalar
        def _(act):
            act.sem_inc(relu_act, 2)
            act.wait_ge(logits_ready, 1)
            act.activation(prob[:, :, :], logit[:, :, :], ACT.Sigmoid).then_inc(prob_ready, 1)
            with act.Fori(0, EXPERTS // 2) as e2:
                for n in range(UNITS):
                    act.wait_ge(out_full, e2 * UNITS + (n + 1))
                    for k in (1, 3):
                        act.wait_ge(hid_full, e2 * (UNITS * HBLK) + (n * HBLK + k + 1))
                        act.sem_inc(passed, 1)
                        act.activation(hid[:, n % 2, k, :], HB[k][:, :], ACT.Relu,
                                       bias=M.b1[:, ds(e2 * (2 * HBLK) + (n // SEQS * HBLK + k), 1)]).then_inc(relu_act, 1)

        @block.vector
        def _(dve):
            dve.sem_inc(relu_dve, 2)
            dve.sem_inc(out_full, 2)
            dve.sem_inc(combined, 2)
            dve.wait_ge(logits_full, 1)
            dve.tensor_tensor(logit[:, :, :], GB[0][:, 0:NTOK // P * EXPERTS].rearrange("p (t e) -> p t e", e=EXPERTS),
                              M.bg[:, :].rearrange("p (o e) -> p o e", o=1).broadcast_to([P, NTOK // P, EXPERTS]),
                              ALU.add).then_inc(logits_ready, 1)
            dve.wait_ge(prob_ready, 1)
            dve.scalar_tensor_tensor(out=gate[:, :, :], in0=logit[:, :, :], scalar=0.0, in1=prob[:, :, :],
                                     op0=ALU.is_gt, op1=ALU.mult).then_inc(gate_ready, 1)
            for s in range(SEQS):
                dve.wait_ge(gate_t_full, s + 1)
                dve.tensor_copy(gate_t[:, s * T:(s + 1) * T], HB[s][0:EXPERTS, :]).then_inc(gate_t_ready, 1)
            for s in range(SEQS):
                dve.wait_ge(bias_full, s + 1)
                dve.tensor_copy(acc[:, s * TILES:(s + 1) * TILES, :],
                                GB[s % 2][:, :].rearrange("p (i d) -> p i d", d=D)).then_inc(bias_copied, 1)
            dve.wait_ge(bias_copied, SEQS)
            with dve.Fori(0, EXPERTS // 2) as e2:
                def relu(n):
                    dve.wait_ge(out_full, e2 * UNITS + (n + 1))
                    for k in (0, 2):
                        dve.wait_ge(hid_full, e2 * (UNITS * HBLK) + (n * HBLK + k + 1))
                        dve.tensor_scalar(hid[:, n % 2, k, :], HB[k][:, :],
                                          M.b1[:, ds(e2 * (2 * HBLK) + (n // SEQS * HBLK + k), 1)], 0.0,
                                          ALU.add, ALU.max).then_inc(relu_dve, 1)

                def combine(n):
                    dve.wait_ge(out_full, e2 * UNITS + (n + 3))
                    dve.wait_ge(combined, e2 * UNITS + (n + 2))
                    for i in range(TILES):
                        t = n % SEQS * TILES + i
                        last = dve.scalar_tensor_tensor(
                            out=acc[:, t, :], in0=YB[n % 2][:, i * D:(i + 1) * D],
                            scalar=gate_cols[:, ds(e2 * 2 + (t * EXPERTS + n // SEQS), 1)],
                            in1=acc[:, t, :], op0=ALU.mult, op1=ALU.add)
                    last.then_inc(combined, 1)

                for n in range(0, UNITS, 2):
                    relu(n)
                    relu(n + 1)
                    combine(n)
                    combine(n + 1)
            for s in range(SEQS):
                dve.wait_ge(back_full, s + 1)
                dve.scalar_tensor_tensor(out=M.x[:, s * T:(s + 1) * T], in0=HB[s][:, :], scalar=0.5,
                                         in1=M.x[:, s * T:(s + 1) * T], op0=ALU.mult, op1=ALU.add).then_inc(x_updated, 1)


def linear_attention_block(nc, M):
    with ExitStack() as ctx:
        sem = stage_semaphores(nc, ctx, "lin")
        sb = lambda n, s, d=F32: ctx.enter_context(nc.sbuf_tensor(f"lin_{n}", s, d))
        qk_full, vo_full, tok_full, tok_copied, copied_qk, copied_vo = (
            sem(n) for n in ("qk_full", "vo_full", "tok_full", "tok_copied", "copied_qk", "copied_vo"))
        gram_full, gram_copied, gvo_full, gvo_copied, mix_full, mix_copied, out_full, x_updated = (
            sem(n) for n in ("gram_full", "gram_copied", "gvo_full", "gvo_copied", "mix_full", "mix_copied",
                             "out_full", "x_updated"))
        HP = LIN_HEADS // 2
        qk = sb("qk", [P, LIN_HEADS * D])
        vo = sb("vo", [P, LIN_HEADS * D])
        tok = sb("tok", [P, NTOK // P, D])
        gram = sb("gram", [P, SEQS * D])
        gvo = sb("gvo", [P, LIN_HEADS, SEQS, D])
        mix = sb("mix", [P, SEQS * D])
        block = ctx.enter_context(nc.Block())
        B = M.bank

        @block.tensor
        def _(pe):
            pe.wait_ge(M.lin_loaded, 16 * M.lin_dmas)
            for j in range(2):
                for c in range(2):
                    for n in range(4):
                        p_ = 4 * c + n
                        mm = pe.matmul(B[2 * j + c][:, n * D:(n + 1) * D], M.wk[64 * j:64 * j + 64, p_ * D:(p_ + 1) * D],
                                       M.wq[64 * j:64 * j + 64, p_ * D:(p_ + 1) * D], start=True, stop=True)
                    mm.then_inc(qk_full, 1)
            for j in range(2):
                for c in range(2):
                    for n in range(4):
                        p_ = 4 * c + n
                        mm = pe.matmul(B[4 + 2 * j + c][:, n * D:(n + 1) * D], M.wv[64 * j:64 * j + 64, p_ * D:(p_ + 1) * D],
                                       M.wo_lin[64 * j:64 * j + 64, p_ * D:(p_ + 1) * D], start=True, stop=True)
                    mm.then_inc(vo_full, 1)
            for s in range(SEQS):
                pe.wait_ge(copied_qk, s + 1)
                for i in range(TILES):
                    mm = pe.transpose(B[s][:, i * P:(i + 1) * P], M.xh[:, (s * TILES + i) * P:(s * TILES + i + 1) * P],
                                      M.ident[:, :])
                mm.then_inc(tok_full, 1)
            pe.wait_ge(copied_vo, 1)
            for s in range(SEQS):
                pe.wait_ge(tok_copied, s + 1)
                for i in range(TILES):
                    mm = pe.matmul(B[4][:, s * D:(s + 1) * D], tok[:, s * TILES + i, :], tok[:, s * TILES + i, :],
                                   start=(i == 0), stop=(i == TILES - 1))
            mm.then_inc(gram_full, 1)
            pe.wait_ge(gram_copied, 1)
            pe.wait_ge(copied_vo, 4)
            for s in range(SEQS):
                for c in range(4):
                    n = 4 * s + c
                    if n >= 4:
                        pe.wait_ge(gvo_copied, n - 3)
                    pe.matmul(B[n % 4][:, :], gram[:, s * D:(s + 1) * D], vo[:, c * T:(c + 1) * T],
                              start=True, stop=True).then_inc(gvo_full, 1)
            pe.wait_ge(gvo_copied, 16)
            for h in range(LIN_HEADS):
                mm = pe.matmul(B[5][:, :], qk[:, h * D:(h + 1) * D], gvo[:, h, :, :].rearrange("p s d -> p (s d)"),
                               start=(h == 0), stop=(h == LIN_HEADS - 1))
            mm.then_inc(mix_full, 1)
            pe.wait_ge(mix_copied, 1)
            for s in range(SEQS):
                pe.matmul(B[s][:, :], mix[:, s * D:(s + 1) * D], M.xh[:, s * T:(s + 1) * T],
                          start=True, stop=True).then_inc(out_full, 1)

        @block.scalar
        def _(act):
            for n in range(4):
                act.wait_ge(vo_full, n + 1)
                act.activation(vo[:, n * T:(n + 1) * T], B[4 + n][:, :], ACT.Copy).then_inc(copied_vo, 1)
            for n in range(0, 16):
                s, c = n // 4, n % 4
                act.wait_ge(gvo_full, n + 1)
                act.activation(gvo[:, 4 * c:4 * c + 4, s, :], B[n % 4][:, :].rearrange("p (h d) -> p h d", d=D),
                               ACT.Copy).then_inc(gvo_copied, 1)

        @block.vector
        def _(dve):
            for n in range(4):
                dve.wait_ge(qk_full, n + 1)
                dve.tensor_copy(qk[:, n * T:(n + 1) * T], B[n][:, :]).then_inc(copied_qk, 1)
            for s in range(SEQS):
                dve.wait_ge(tok_full, s + 1)
                dve.tensor_copy(tok[:, s * TILES:(s + 1) * TILES, :],
                                B[s][:, :].rearrange("p (i d) -> p i d", d=D)).then_inc(tok_copied, 1)
            dve.wait_ge(gram_full, 1)
            dve.tensor_copy(gram[:, :], B[4][:, :]).then_inc(gram_copied, 1)
            dve.wait_ge(mix_full, 1)
            dve.tensor_scalar(mix[:, :], B[5][:, :], LIN_DK ** -0.5, None, ALU.mult).then_inc(mix_copied, 1)
            for s in range(SEQS):
                dve.wait_ge(out_full, s + 1)
                dve.tensor_tensor(M.x[:, s * T:(s + 1) * T], M.x[:, s * T:(s + 1) * T], B[s][:, :],
                                  ALU.add).then_inc(x_updated, 1)


def local_transformer_block(nc, M, W, name):
    with ExitStack() as ctx:
        sem = stage_semaphores(nc, ctx, name)
        sb = lambda n, s, d=F32: ctx.enter_context(nc.sbuf_tensor(f"{name}_{n}", s, d))
        proj_full, squared, v_ready, rotated, qk_ready, turned_full, turned_ready = (
            sem(n) for n in ("proj_full", "squared", "v_ready", "rotated", "qk_ready", "turned_full", "turned_ready"))
        score_full, max_ready, exp_done, recip_ready, prob_ready, pt_full = (
            sem(n) for n in ("score_full", "max_ready", "exp_done", "recip_ready", "prob_ready", "pt_full"))
        pt_ready = [sem("pt_ready_even"), sem("pt_ready_odd")]
        out_full, out_ready, y_full, z_attn = (sem(n) for n in ("out_full", "out_ready", "y_full", "z_attn"))
        passed, pe_passed = sem("passed"), sem("pe_passed")
        prev_loaded = [sem("prev_loaded_even"), sem("prev_loaded_odd")]
        xa_first, xa_rest, shifted_ffn, tables_ready, norm_step, sum_ready = (
            sem(n) for n in ("xa_first", "xa_rest", "shifted_ffn", "tables_ready", "norm_step", "sum_ready"))
        mean_full, centred, sqf_ready, var_full, rstd_step, rstd_full, xn_scaled, xn_ready = (
            sem(n) for n in ("mean_full", "centred", "sqf_ready", "var_full", "rstd_step", "rstd_full",
                             "xn_scaled", "xn_ready"))
        gate_full, gelu_done, lin_full, hid_ready, ffn_full, z_ffn = (
            sem(n) for n in ("gate_full", "gelu_done", "lin_full", "hid_ready", "ffn_full", "z_ffn"))
        qkv_loaded, rest_loaded, vec_loaded, cleared, x_added = (
            sem(n) for n in ("qkv_loaded", "rest_loaded", "vec_loaded", "cleared", "x_added"))

        z = M.z
        xa_bits, xa_high, xa_low = sb("xa_bits", [P, T]), sb("xa_high", [P, T], F32R), sb("xa_low", [P, T], F32R)
        xs = sb("xs", [P, SEQS * T])
        wqkv = sb("wqkv", [P, 3 * INNER])
        w_bits = sb("w_bits", [P, 2, T])
        wqkv_high, wqkv_low = sb("wqkv_high", [P, 3 * INNER], F32R), sb("wqkv_low", [P, 3 * INNER], F32R)
        bits_done, w_bits_done, w_high, w_ready = sem("bits_done"), sem("w_bits_done"), sem("w_high"), sem("w_ready")
        wo = sb("wo", [P, PAIRS * D])
        w1 = sb("w1", [P, 2 * FF])
        w2 = sb("w2", [P, FBLK * D])
        vec = sb("vec", [P, 3 * FBLK])
        scales = sb("scales", [P, 4, DH])
        rot = sb("rot", [P, 4, TILES, DH])
        sq = sb("sq", [P, 2, T])
        rc = sb("rc", [P, 4, T])
        rs = sb("rs", [P, 2, T])
        qk = sb("qk", [P, 2, T])
        ssq = sb("ssq", [P, 2, 16])
        rn = sb("rn", [P, 2, 16])
        rt = sb("rt", [P, 2, 16])
        qT = sb("qT", [P, 2, PAIRS, 2, P])
        kT = sb("kT", [P, PAIRS, WINDOW + T])
        V = sb("V", [P, 2, INNER])
        Vp = sb("Vp", [P, 2, PAIRS, P])
        negmax = sb("negmax", [P, 4, 2])
        total = sb("total", [P, 4, 2])
        recip = sb("recip", [P, 4, 2])
        prob = sb("prob", [P, GROUPS, 4, KEYS])
        prob_prev = sb("prob_prev", [P, GROUPS, 4, WINDOW])
        PT = sb("PT", [P, 2, 4, P])
        PTp = sb("PTp", [P, 2, P])
        outT = sb("outT", [P, PAIRS, P])
        xc = sb("xc", [P, 2, T])
        var, rstd, vt = (sb(n, [P, 2, TILES]) for n in ("var", "rstd", "vt"))
        xn = sb("xn", [P, 2, T])
        gg = sb("gg", [P, FBLK, T])
        hid = sb("hid", [P, FBLK, T])
        block = ctx.enter_context(nc.Block())
        PJ, TQ, SC, PTB, PX, OT = M.bank[0:2], M.bank[2], M.bank[3:5], M.bank[5], M.bank[6], M.bank[7]

        def at(n, per_tile, tile, k):
            return n * (TILES * per_tile) + (tile * per_tile + k + CREDIT * per_tile + 1)

        def prev_count(n, j):
            return n * (64 * ((TILES - 1 + j % 2) // 2)) + 64 * ((j + 1) // 2)

        PROJ = ["k0", "q0", "k1", "v0", "q1", "v1"]
        ROT = ["k0", "q0", "k1", "q1"]
        COL = {"q": 0, "k": INNER, "v": 2 * INNER}
        PLAN = [[(1, "q0")],
                [(0, "Tk1"), (1, "k1"), (0, "Tq1")],
                [(1, "v0"), (1, "q1")],
                [(1, "Tk0"), (1, "v1"), (1, "Tq0"), (2, "k0")]]
        PROLOGUE = [(0, w) for w in ("k0", "q0", "k1", "v0", "q1", "Tk0", "v1", "Tq0")] + [(1, "k0")]

        def schedule(first, last):
            slots = [(i, g) for i in range(TILES) for g in range(GROUPS)]

            def late(n, k):
                if n - k < 0:
                    return None if first else (-1, GROUPS + n - k)
                return slots[n - k] if n - k < len(slots) else None
            for n in range(len(slots) + (3 if last else 0)):
                now = slots[n] if n < len(slots) else None
                pieces = [(now[0] + d, w) for d, w in PLAN[now[1]] if not (last and now[0] + d >= TILES)] if now else []
                y = late(n, 3)
                yield now, pieces, late(n, 1), late(n, 2), y[0] if y and y[1] == GROUPS - 1 else None

        def turned_probs(n, j, g):
            j, g = (j, g) if g >= 0 else (j - 1, g + GROUPS)
            return pt_ready[g % 2], at(n, 2, j, g // 2 + 1)

        def sequences(eng, layer, body):
            body(0, layer * SEQS, True, False)
            with eng.Fori(1, SEQS - 1) as s:
                body(s, layer * SEQS + s, False, False)
            body(SEQS - 1, layer * SEQS + (SEQS - 1), False, True)

        @block.sync
        def _(sp):
            def load_projections(L):
                sp.wait_ge(proj_full, at(L * SEQS, 6, -1, 6))
                sp.dma_start(wqkv[:, :], W["wqkv"][ds(L, 1), :, :].rearrange("o p n -> p (o n)")).then_inc(qkv_loaded, 16)
                sp.wait_ge(tables_ready, L * 4 + 1)
                sp.dma_start(scales[:, :, :],
                             W["scales"][ds(L, 1), :].broadcast_to([P, 4 * DH]).rearrange("p (a d) -> p a d", d=DH)
                             ).then_inc(qkv_loaded, 16)

            load_projections(0)
            with sp.Fori(0, DEPTH) as L:
                sp.wait_ge(z_ffn, L * SEQS + 1)
                sp.dma_start(wo[:, :], W["wo"][ds(L, 1), :, :].rearrange("o p n -> p (o n)")).then_inc(rest_loaded, 16)
                sp.dma_start(w1[:, :], W["w1"][ds(L, 1), :, :].rearrange("o p n -> p (o n)")).then_inc(rest_loaded, 16)
                sp.dma_start(w2[:, :], W["w2"][ds(L, 1), :, :].rearrange("o p n -> p (o n)")).then_inc(rest_loaded, 16)
                sp.dma_start(vec[:, :], W["vec"][ds(L, 1), :, :].rearrange("o p n -> p (o n)")).then_inc(rest_loaded, 16)
                with sp.Fori(0, SEQS) as s:
                    n = L * SEQS + s
                    for j in range(TILES - 1):
                        sp.wait_ge(v_ready, at(n, 2, j, 2))
                        sp.sem_inc(passed, 1)
                        sp.wait_ge(out_full, at(n, 4, j - 1, 4))
                        for r in range(4):
                            e, c = r // 2, r % 2
                            src = V[P - WINDOW:P, j % 2, :].rearrange("p (q e c d) -> p q e c d", e=2, c=2, d=DH)[:, :, e, c, :]
                            dst = Vp[32 * r:32 * r + 32, (j + 1) % 2, :, :].rearrange(
                                "p (q e) (c d) -> p q e c d", e=2, c=2)[:, :, e, c, :]
                            sp.dma_start(dst, src).then_inc(prev_loaded[(j + 1) % 2], 16)
                load_projections(L + 1)

        @block.tensor
        def _(pe):
            def proj(n, j, what):
                idx = PROJ.index(what)
                if idx == 0:
                    pe.wait_ge(rotated, at(n, 4, j - 1, 4))
                elif idx == 1:
                    pe.wait_ge(v_ready, at(n, 2, j - 1, 2))
                elif idx == 5:
                    pe.wait_ge(v_ready, at(n, 2, j, 1))
                else:
                    pe.wait_ge(rotated, at(n, 4, j, idx - 1))
                col = COL[what[0]] + int(what[1]) * T
                tile = slice(j % TILES * P, (j % TILES + 1) * P)
                w_cols = slice(col, col + T)
                pe.matmul(PJ[idx % 2][:, :], xa_high[:, tile], wqkv_low[:, w_cols], start=True, stop=False)
                pe.matmul(PJ[idx % 2][:, :], xa_low[:, tile], wqkv_high[:, w_cols], start=False, stop=False)
                pe.matmul(PJ[idx % 2][:, :], xa_high[:, tile], wqkv_high[:, w_cols],
                          start=False, stop=True).then_inc(proj_full, 1)

            def turn_qk(n, j, what):
                f = ROT.index(what[1:])
                pe.wait_ge(qk_ready, at(n, 4, j, f + 1))
                pe.wait_ge(turned_ready, at(n, 4, j, f))
                for c in range(4):
                    mm = pe.transpose(TQ[:, c * P:(c + 1) * P], qk[:, f % 2, c * P:(c + 1) * P], M.ident[:, :])
                mm.then_inc(turned_full, 1)

            def pieces(n, todo):
                for j, what in todo:
                    if what[0] == "T":
                        turn_qk(n, j, what)
                    else:
                        if what == "k0" and j == TILES:
                            pe.wait_ge(xa_first, n + 2)
                        if what == "k0" and j % TILES == 1:
                            pe.wait_ge(xa_rest, n + 1 + j // TILES)
                        proj(n, j, what)

            def scores(n, j, p):
                if p == 0:
                    pe.wait_ge(turned_ready, at(n, 4, j, 2))
                if p == PAIRS // 2:
                    pe.wait_ge(turned_ready, at(n, 4, j, 4))
                pe.wait_ge(exp_done, at(n, 8, j, p - 1))
                bank = SC[p % 2]
                pe.matmul(bank[:, 0:2 * KEYS], M.ident16[:, :], M.mask[:, int(j > 0), :],
                          start=True, stop=False, skip_group_check=True)
                for c in range(2):
                    mm = pe.matmul(bank[:, c * KEYS:(c + 1) * KEYS], qT[:, j % 2, p, c, :], kT[:, p, j * P:j * P + KEYS],
                                   start=False, stop=(c == 1), skip_group_check=True)
                mm.then_inc(score_full, 1)

            def turn_probs(n, j, g):
                pe.wait_ge(prob_ready, at(n, 8, j, 2 * g + 2))
                pe.wait_ge(*turned_probs(n, j, g - 1))
                for h in range(4):
                    pe.transpose(PTB[:, h * P:(h + 1) * P], prob[:, g, h, WINDOW:KEYS], M.ident[:, :])
                pe.transpose(PX[:, 0:P], prob_prev[:, g, :, :].rearrange("p h k -> p (h k)"), M.ident[:, :]).then_inc(pt_full, 1)

            def values(n, j, g):
                pe.wait_ge(*turned_probs(n, j, g))
                if g == 0:
                    pe.wait_ge(z_attn, at(n, 1, j - 1, 1))
                    if j > 0:
                        pe.wait_ge(prev_loaded[j % 2], prev_count(n, j))
                else:
                    pe.wait_ge(out_ready, at(n, 4, j, g))
                if g % 2 == 0:
                    pe.wait_ge(v_ready, at(n, 2, j, g // 2 + 1))
                for pp in range(2):
                    p = 2 * g + pp
                    pe.matmul(OT[:, pp * P:(pp + 1) * P], Vp[:, j % 2, p, :], PTp[:, g % 2, :],
                              start=True, stop=False, skip_group_check=True)
                    for c in range(2):
                        mm = pe.matmul(OT[64 * c:64 * c + 64, pp * P:(pp + 1) * P],
                                       V[:, j % 2, (2 * p + c) * DH:(2 * p + c + 1) * DH],
                                       PT[:, g % 2, 2 * pp + c, :], start=False, stop=True, skip_group_check=True)
                mm.then_inc(out_full, 1)

            def output(n, j):
                pe.wait_ge(out_ready, at(n, 4, j, 4))
                for p in range(PAIRS):
                    mm = pe.matmul(OT[:, 0:P], wo[:, p * D:(p + 1) * D], outT[:, p, :],
                                   start=(p == 0), stop=(p == PAIRS - 1))
                mm.then_inc(y_full, 1)

            def mean(n, s):
                pe.wait_ge(shifted_ffn, n + s + 1)
                if s == 0:
                    pe.wait_ge(rotated, at(n + SEQS, 4, -1, 4))
                if s >= 2:
                    pe.wait_ge(z_ffn, n + s - 1 + 1)
                pe.matmul(PJ[0][:, :], M.mean_w[:, :], xs[:, s * T:(s + 1) * T],
                          start=True, stop=True).then_inc(mean_full, 1)

            def variance(n, s):
                pe.wait_ge(sqf_ready, n + s + 1)
                if s == 0:
                    pe.wait_ge(v_ready, at(n + SEQS, 2, -1, 2))
                else:
                    pe.wait_ge(xn_scaled, n + s)
                for i in range(TILES):
                    mm = pe.matmul(PJ[1][:, i:i + 1], sq[:, s % 2, i * P:(i + 1) * P], M.mean_w[:, 0:1],
                                   start=True, stop=True)
                mm.then_inc(var_full, 1)

            def spread(n, s):
                pe.wait_ge(rstd_step, (n + s) * NEWTON + NEWTON)
                for i in range(TILES):
                    mm = pe.matmul(PJ[1][:, i * P:(i + 1) * P], rstd[:, s % 2, i:i + 1].broadcast_to([P, P]),
                                   M.ident[:, :], start=True, stop=True)
                mm.then_inc(rstd_full, 1)

            def hidden(n, s, base, banks, used, full):
                for k in range(FBLK):
                    pe.wait_ge(used, n * FBLK + (s * FBLK + k + 1))
                    pe.matmul(banks[k][0:blk(k), :], w1[:, base + k * P:base + k * P + blk(k)], xn[:, s % 2, :],
                              start=True, stop=True).then_inc(full, 1)

            def gates(n, s):
                pe.wait_ge(xn_ready, n + s + 1)
                if s == 0:
                    pe.wait_ge(turned_ready, at(n + SEQS, 4, -1, 4))
                    pe.wait_ge(exp_done, at(n + SEQS, 8, -1, 8))
                hidden(n, s, FF, [SC[0], SC[1], TQ], gelu_done, gate_full)

            def sequence(s, n, first, last):
                for now, todo, turn, value, y in schedule(first, last):
                    if now:
                        scores(n, now[0], 2 * now[1])
                        scores(n, now[0], 2 * now[1] + 1)
                    if y is not None:
                        output(n, y)
                    late_piece = todo[-1:] if now and now[1] in (2, 3) else []
                    pieces(n, todo[:len(todo) - len(late_piece)])
                    if last and now == (TILES - 1, 0):
                        mean(n - (SEQS - 1), 0)
                    if last and now == (TILES - 1, 1):
                        variance(n - (SEQS - 1), 0)
                    if last and now == (TILES - 1, 3):
                        spread(n - (SEQS - 1), 0)
                    if turn:
                        turn_probs(n, *turn)
                    if turn == (TILES - 1, GROUPS - 1):
                        gates(n - (SEQS - 1), 0)
                    if value:
                        values(n, *value)
                    pieces(n, late_piece)

            def begin(L, todo):
                pe.wait_ge(xa_rest, L * SEQS + 1)
                for j, what in todo:
                    if what[0] != "T" and j == 0:
                        pe.wait_ge(w_ready, L * len(PROJ) + (PROJ.index(what) + 1))
                    pieces(L * SEQS, [(j, what)])

            def feed_forward(L):
                n = L * SEQS
                for turned in pt_ready:
                    pe.wait_ge(turned, at(n + SEQS, 2, -1, 2))
                pe.wait_ge(z_attn, at(n + SEQS, 1, -1, 1))
                for s in range(SEQS):
                    if s + 1 < SEQS:
                        mean(n, s + 1)
                    if s > 0:
                        gates(n, s)
                    if s + 1 < SEQS:
                        variance(n, s + 1)
                    final = s + 1 == SEQS
                    if final:
                        pe.wait_ge(z_ffn, n + s + 1)
                        begin(L + 1, PROLOGUE[:1])
                    hidden(n, s, 0, [PTB, PX, OT], hid_ready, lin_full)
                    if s + 1 < SEQS:
                        spread(n, s + 1)
                        pe.wait_ge(centred, n + s + 2)
                    if final:
                        pe.wait_ge(xn_scaled, n + SEQS)
                        begin(L + 1, PROLOGUE[1:2])
                    for k in range(FBLK):
                        pe.wait_ge(hid_ready, n * FBLK + (s * FBLK + k + 1 + FBLK))
                        mm = pe.matmul((SC if final else PJ)[0][:, :], w2[0:blk(k), k * D:(k + 1) * D], hid[0:blk(k), k, :],
                                       start=(k == 0), stop=(k == FBLK - 1))
                    mm.then_inc(ffn_full, 1)
                begin(L + 1, PROLOGUE[2:])

            pe.wait_ge(cleared, 5)
            begin(0, PROLOGUE)
            with pe.Fori(0, DEPTH) as L:
                pe.wait_ge(z_ffn, L * SEQS + 1)
                pe.wait_ge(rest_loaded, L * 64 + 64)
                sequences(pe, L, sequence)
                feed_forward(L)

        @block.scalar
        def _(act):
            sem_start(act, [(squared, 4), (v_ready, 2), (turned_ready, 4), (exp_done, 8), (out_ready, 4),
                            (pt_ready[0], 2)])
            act.sem_inc(gelu_done, FBLK)

            def pieces(n, todo):
                for j, what in todo:
                    if what[0] == "T":
                        name_, grp = what[1], int(what[2])
                        act.wait_ge(turned_full, at(n, 4, j, ROT.index(what[1:]) + 1))
                        src = TQ[:, :].rearrange("p (c t) -> p c t", t=P)
                        if name_ == "q":
                            act.activation(qT[0:64, j % 2, 4 * grp:4 * grp + 4, 0, :], src[0:64], ACT.Copy)
                            act.activation(qT[64:P, j % 2, 4 * grp:4 * grp + 4, 1, :], src[64:P],
                                           ACT.Copy).then_inc(turned_ready, 1)
                        else:
                            c0 = WINDOW + (j % TILES) * P
                            act.activation(kT[:, 4 * grp:4 * grp + 4, c0:c0 + P], src, ACT.Copy).then_inc(turned_ready, 1)
                        continue
                    idx = PROJ.index(what)
                    act.wait_ge(proj_full, at(n, 6, j, idx + 1))
                    if what[0] == "v":
                        if what == "v0":
                            act.wait_ge(out_full, at(n, 4, j - 2, 4))
                            if j >= 2:
                                act.wait_ge(prev_loaded[(j - 1) % 2], prev_count(n, j - 1))
                        g = int(what[1])
                        act.activation(V[:, j % 2, g * T:(g + 1) * T], PJ[idx % 2][:, :], ACT.Copy).then_inc(v_ready, 1)
                    else:
                        f = ROT.index(what)
                        act.wait_ge(rotated, at(n, 4, j, f - 1))
                        act.activation(sq[:, f % 2, :], PJ[idx % 2][:, :], ACT.Square).then_inc(squared, 1)

            def exponentials(n, j, p):
                g = p // 2
                act.wait_ge(pt_full, at(n, 4, j - 1, g + 1))
                act.wait_ge(max_ready, at(n, 8, j, p + 1))
                act.wait_ge(recip_ready, at(n, 8, j, p - 3))
                for c in range(2):
                    last = act.activation(prob[:, g, 2 * (p % 2) + c, :], SC[p % 2][:, c * KEYS:(c + 1) * KEYS],
                                          ACT.Exp, bias=negmax[:, p % 4, c:c + 1],
                                          accum_out=total[:, p % 4, c:c + 1])
                last.then_inc(exp_done, 1)

            def square(n, s):
                act.wait_ge(centred, n + s + 1)
                if s >= 2:
                    act.wait_ge(var_full, n + s - 1)
                act.activation(sq[:, s % 2, :], xc[:, s % 2, :], ACT.Square).then_inc(sqf_ready, 1)

            def sequence(s, n, first, last):
                for now, todo, turn, value, y in schedule(first, last):
                    if value and value[1] % 2 == 0:
                        j, g = value
                        act.wait_ge(pt_full, at(n, 4, j, g + 1))
                        act.wait_ge(out_full, at(n, 4, j, g - 1))
                        act.activation(PT[:, g % 2, :, :], PTB[:, :].rearrange("p (h t) -> p h t", t=P), ACT.Copy)
                        act.activation(PTp[:, g % 2, :], PX[:, 0:P], ACT.Copy).then_inc(pt_ready[0], 1)
                    turned = [p for p in todo if p[1][0] == "T"]
                    pieces(n, turned[:1])
                    if now:
                        exponentials(n, now[0], 2 * now[1])
                        exponentials(n, now[0], 2 * now[1] + 1)
                    pieces(n, turned[1:])
                    pieces(n, [p for p in todo if p[1][0] != "T"])
                    if last and now == (TILES - 1, 0):
                        square(n - (SEQS - 1), 0)
                    if value:
                        j, g = value
                        act.wait_ge(out_full, at(n, 4, j, g + 1))
                        if g == 0:
                            act.wait_ge(y_full, at(n, 1, j - 1, 1))
                        act.activation(outT[:, 2 * g:2 * g + 2, :], OT[:, 0:2 * P].rearrange("p (c t) -> p c t", t=P),
                                       ACT.Copy).then_inc(out_ready, 1)

            def feed_forward(L):
                n = L * SEQS

                for s in range(SEQS):
                    if s + 1 < SEQS:
                        square(n, s + 1)
                    for k in range(FBLK):
                        act.wait_ge(gate_full, n * FBLK + (s * FBLK + k + 1))
                        act.wait_ge(hid_ready, n * FBLK + (s * FBLK + k + 1))
                        act.activation(gg[0:blk(k), k, :], [SC[0], SC[1], TQ][k][0:blk(k), :], ACT.Gelu,
                                       bias=vec[0:blk(k), FBLK + k:FBLK + k + 1]).then_inc(gelu_done, 1)

            pieces(0, PROLOGUE)
            with act.Fori(0, DEPTH) as L:
                sequences(act, L, sequence)
                act.wait_ge(rest_loaded, L * 64 + 64)
                feed_forward(L)
                pieces((L + 1) * SEQS, PROLOGUE)

        @block.gpsimd
        def _(pool):
            sem_start(pool, [(qk_ready, 4), (sum_ready, 4), (prob_ready, 8), (proj_full, 6), (turned_full, 4), (score_full, 8),
                             (pt_full, 4), (out_full, 4), (y_full, 1)])
            pool.memset(Vp[:, :, :, :], 0.0).then_inc(cleared, 1)
            pool.memset(kT[:, :, :], 0.0).then_inc(cleared, 1)
            pool.memset(qT[:, :, :, :, :], 0.0).then_inc(cleared, 1)
            pool.memset(xs[:, :], 0.0).then_inc(cleared, 1)
            pool.memset(xa_bits[:, :], 0.0).then_inc(cleared, 1)

            def add(n, j, what):
                f = ROT.index(what)
                pool.wait_ge(rotated, at(n, 4, j, f + 1))
                pool.tensor_tensor(rc[:, f, :], rc[:, f, :], rs[:, f % 2, :], ALU.add).then_inc(sum_ready, 1)

            def scale(n, j, what):
                f = ROT.index(what)
                pool.wait_ge(sum_ready, at(n, 4, j, f + 1))
                pool.wait_ge(norm_step, n * (2 * TILES * NEWTON) + (2 * j + f // 2 + 1) * NEWTON)
                pool.wait_ge(turned_full, at(n, 4, j, f - 1))
                pool.tensor_tensor(qk[:, f % 2, :].rearrange("p (h d) -> p h d", d=DH),
                                   rc[:, f, :].rearrange("p (h d) -> p h d", d=DH),
                                   rn[:, f // 2, 8 * (f % 2):8 * (f % 2) + 8].rearrange("p (h o) -> p h o", o=1)
                                   .broadcast_to([P, 8, DH]), ALU.mult).then_inc(qk_ready, 1)

            def normalise(n, j, p):
                pool.wait_ge(recip_ready, at(n, 8, j, p + 1))
                two = slice(2 * (p % 2), 2 * (p % 2) + 2)
                by = recip[:, p % 4, :].rearrange("p (h o) -> p h o", o=1)
                pool.tensor_tensor(prob_prev[:, p // 2, two, :], prob[:, p // 2, two, 0:WINDOW],
                                   by.broadcast_to([P, 2, WINDOW]), ALU.mult)
                v = prob[:, p // 2, two, WINDOW:KEYS]
                pool.tensor_tensor(v, v, by.broadcast_to([P, 2, P]), ALU.mult).then_inc(prob_ready, 1)

            def sequence(s, n, first, last):
                for now, todo, turn, value, y in schedule(first, last):
                    if not now:
                        continue
                    j, g = now
                    following = not (last and j == TILES - 1)
                    if g == 0:
                        scale(n, j, "k1")
                        scale(n, j, "q1")
                    if g == 2 and following:
                        scale(n, j + 1, "k0")
                        scale(n, j + 1, "q0")
                    normalise(n, j, 2 * g)
                    normalise(n, j, 2 * g + 1)
                    if following:
                        add(n, j + 1, ROT[g])

            def begin(L):
                for k, what in enumerate(PROJ):
                    cols = slice(COL[what[0]] + int(what[1]) * T, COL[what[0]] + int(what[1]) * T + T)
                    pool.wait_ge(w_high, L * len(PROJ) + (k + 1))
                    pool.tensor_tensor(wqkv_low[:, cols], wqkv[:, cols], w_bits[:, k % 2, :],
                                       ALU.subtract).then_inc(w_ready, 1)
                for w in ("k0", "q0"):
                    add(L * SEQS, 0, w)
                for w in ("k0", "q0"):
                    scale(L * SEQS, 0, w)
                for w in ("k1", "q1"):
                    add(L * SEQS, 0, w)

            begin(0)
            with pool.Fori(0, DEPTH) as L:
                sequences(pool, L, sequence)
                begin(L + 1)

        @block.vector
        def _(dve):
            sem_start(dve, [(rotated, 4), (max_ready, 8), (recip_ready, 8), (pt_ready[1], 2), (z_attn, 1)])
            dve.sem_inc(z_ffn, 1)
            dve.sem_inc(hid_ready, FBLK)
            dve.sem_inc(tables_ready, 1)
            dve.wait_ge(cleared, 5)

            def shift(s):
                dve.tensor_copy(xs[0:64, ds(s * T, T)], z[0:64, ds(s * T, T)])
                dve.tensor_copy(xs[64:P, ds(s * T + 1, T - 1)], z[64:P, ds(s * T, T - 1)]).then_inc(shifted_ffn, 1)

            def split(s, lo, hi, count, ready):
                late = max(lo, 1)
                moves = [(slice(0, 64), slice(lo, hi), ds(s * T + lo, hi - lo)),
                         (slice(64, P), slice(late, hi), ds(s * T + (late - 1), hi - late))]
                for rows, to, of in moves:
                    last = dve.tensor_scalar(xa_bits[rows, to].bitcast(I32), z[rows, of].bitcast(I32),
                                             LOW_BITS, None, ALU.bitwise_and)
                last.then_inc(bits_done, 1)
                dve.wait_ge(bits_done, count)
                dve.tensor_copy(xa_high[:, lo:hi], xa_bits[:, lo:hi])
                for rows, to, of in moves:
                    last = dve.tensor_tensor(xa_low[rows, to], z[rows, of], xa_bits[rows, to], ALU.subtract)
                last.then_inc(ready, 1)

            def shift_first(s, m):
                split(s, 0, P, m * 2 + 1, xa_first)

            def shift_rest(s, m):
                split(s, P, T, m * 2 + 2, xa_rest)

            dve.tensor_copy(xa_low[64:P, 0:1], xa_bits[64:P, 0:1])
            shift_first(0, 0)
            shift_rest(0, 0)

            def rotate(n, j, what):
                f, idx = ROT.index(what), PROJ.index(what)
                c = 0 if what[0] == "q" else 2
                bank, tile = PJ[idx % 2], j % TILES
                dve.wait_ge(squared, at(n, 4, j, f + 1))
                dve.wait_ge(qk_ready, at(n, 4, j - 1, f + 1))
                dve.wait_ge(sum_ready, at(n, 4, j, f - 1))
                tab = lambda a, lo, n_: rot[:, a, tile, lo:lo + n_].rearrange("p (o d) -> p o d", o=1)
                dve.tensor_tensor(rc[:, f, :].rearrange("p (h d) -> p h d", d=DH),
                                  bank[:, :].rearrange("p (h d) -> p h d", d=DH),
                                  tab(c, 0, DH).broadcast_to([P, 8, DH]), ALU.mult)
                for half in range(2):
                    dve.tensor_tensor(
                        rs[:, f % 2, :].rearrange("p (h a d) -> p h a d", a=2, d=DH // 2)[:, :, half, :],
                        bank[:, :].rearrange("p (h a d) -> p h a d", a=2, d=DH // 2)[:, :, 1 - half, :],
                        tab(c + 1, half * (DH // 2), DH // 2).broadcast_to([P, 8, DH // 2]), ALU.mult)
                dve.tensor_reduce(ssq[:, f // 2, 8 * (f % 2):8 * (f % 2) + 8],
                                  sq[:, f % 2, :].rearrange("p (h d) -> p h d", d=DH), AX_X, ALU.add).then_inc(rotated, 1)

            def norms(n, j, h):
                dve.wait_ge(rotated, at(n, 4, j, 2 * h + 2))
                dve.wait_ge(qk_ready, at(n, 4, j - 1, 2 * h + 2))
                inverse_sqrt(dve, norm_step, n * (2 * TILES * NEWTON) + (2 * j + h) * NEWTON, ssq[:, h, :], ssq[:, h, :],
                             rn[:, h, :], rt[:, h, :], ALU.max, 1e-24)

            def maximum(n, j, p):
                dve.wait_ge(score_full, at(n, 8, j, p + 1))
                dve.wait_ge(exp_done, at(n, 8, j, p - 3))
                dve.tensor_reduce(negmax[:, p % 4, :], SC[p % 2][:, 0:2 * KEYS].rearrange("p (h k) -> p h k", k=KEYS),
                                  AX_X, ALU.max, negate=True).then_inc(max_ready, 1)

            def reciprocal(n, j, p):
                dve.wait_ge(exp_done, at(n, 8, j, p + 1))
                dve.wait_ge(prob_ready, at(n, 8, j, p - 3))
                dve.reciprocal(recip[:, p % 4, :], total[:, p % 4, :]).then_inc(recip_ready, 1)

            def copy_probs(n, j, g):
                dve.wait_ge(pt_full, at(n, 4, j, g + 1))
                dve.wait_ge(out_full, at(n, 4, j, g - 1))
                dve.tensor_copy(PT[:, g % 2, :, :], PTB[:, :].rearrange("p (h t) -> p h t", t=P))
                dve.tensor_copy(PTp[:, g % 2, :], PX[:, 0:P]).then_inc(pt_ready[1], 1)

            def centre(n, s):
                dve.wait_ge(mean_full, n + s + 1)
                dve.wait_ge(shifted_ffn, n + s + 1)
                dve.tensor_tensor(xc[:, s % 2, :], xs[:, s * T:(s + 1) * T], PJ[0][:, :],
                                  ALU.subtract).then_inc(centred, 1)

            def deviation(n, s):
                dve.wait_ge(var_full, n + s + 1)
                inverse_sqrt(dve, rstd_step, (n + s) * NEWTON, PJ[1][:, 0:TILES], var[:, s % 2, :],
                             rstd[:, s % 2, :], vt[:, s % 2, :], ALU.add, LN_EPS)

            def normal(n, s):
                dve.wait_ge(rstd_full, n + s + 1)
                if s >= 2:
                    dve.wait_ge(lin_full, n * FBLK + FBLK * (s - 1))
                dve.tensor_tensor(xn[:, s % 2, :], xc[:, s % 2, :], PJ[1][:, :], ALU.mult).then_inc(xn_scaled, 1)
                dve.wait_ge(xn_scaled, n + s + 1)
                dve.tensor_scalar(xn[:, s % 2, :], xn[:, s % 2, :], vec[:, 2 * FBLK + 1:2 * FBLK + 2],
                                  vec[:, 2 * FBLK + 2:2 * FBLK + 3], ALU.mult, ALU.add).then_inc(xn_ready, 1)

            def sequence(s, n, first, last):
                for now, todo, turn, value, y in schedule(first, last):
                    if now == (1, 0) and not last:
                        dve.wait_ge(proj_full, at(n, 6, 0, 6))
                        shift_first(s + 1, n + 1)
                    if now == (3, 0) and not last:
                        dve.wait_ge(proj_full, at(n, 6, TILES - 1, 6))
                        shift_rest(s + 1, n + 1)
                    following = now and not (last and now[0] == TILES - 1)
                    if value and value[1] % 2 == 1:
                        copy_probs(n, *value)
                    if now:
                        maximum(n, now[0], 2 * now[1])
                        maximum(n, now[0], 2 * now[1] + 1)
                    if following:
                        rotate(n, now[0] + 1, ROT[now[1]])
                    if y is not None:
                        dve.wait_ge(y_full, at(n, 1, y, 1))
                        cols = ds(s * T + y * P, P)
                        dve.tensor_tensor(z[:, cols], z[:, cols], OT[:, 0:P], ALU.add).then_inc(z_attn, 1)
                    if now:
                        reciprocal(n, now[0], 2 * now[1])
                        reciprocal(n, now[0], 2 * now[1] + 1)
                    if following and now[1] % 2 == 1:
                        norms(n, now[0] + 1, now[1] // 2)
                    if last and now == (TILES - 1, 0):
                        centre(n - (SEQS - 1), 0)
                    if last and now == (TILES - 1, 2):
                        deviation(n - (SEQS - 1), 0)
                    if last and now == (TILES - 1, 3):
                        normal(n - (SEQS - 1), 0)
                    if y == -1 or (last and y == TILES - 1):
                        dve.wait_ge(z_attn, at(n, 1, y, 1))
                        shift(s if y >= 0 else s - 1)

            def factors(L):
                dve.wait_ge(qkv_loaded, L * 32 + 32)
                for a in range(4):
                    dve.tensor_tensor(rot[:, a, :, :], M.tables[:, a, :, :],
                                      scales[:, a, :].rearrange("p (o d) -> p o d", o=1).broadcast_to([P, TILES, DH]),
                                      ALU.mult).then_inc(tables_ready, 1)
                dve.wait_ge(tables_ready, L * 4 + 5)

            def split_weights(L, blocks):
                for what in blocks:
                    k = PROJ.index(what)
                    cols = slice(COL[what[0]] + int(what[1]) * T, COL[what[0]] + int(what[1]) * T + T)
                    if k >= 2:
                        dve.wait_ge(w_ready, L * len(PROJ) + (k - 1))
                    dve.tensor_scalar(w_bits[:, k % 2, :].bitcast(I32), wqkv[:, cols].bitcast(I32),
                                      LOW_BITS, None, ALU.bitwise_and).then_inc(w_bits_done, 1)
                    dve.wait_ge(w_bits_done, L * len(PROJ) + (k + 1))
                    dve.tensor_copy(wqkv_high[:, cols], w_bits[:, k % 2, :]).then_inc(w_high, 1)

            def feed_forward(L):
                n = L * SEQS

                for s in range(SEQS):
                    if s + 1 < SEQS:
                        centre(n, s + 1)
                        deviation(n, s + 1)
                    for k in range(FBLK):
                        dve.wait_ge(lin_full, n * FBLK + (s * FBLK + k + 1))
                        dve.wait_ge(gelu_done, n * FBLK + (s * FBLK + k + 1 + FBLK))
                        if k == 0:
                            dve.wait_ge(ffn_full, n + s + 1)
                        dve.scalar_tensor_tensor(out=hid[0:blk(k), k, :], in0=[PTB, PX, OT][k][0:blk(k), :],
                                                 scalar=vec[0:blk(k), k:k + 1], in1=gg[0:blk(k), k, :],
                                                 op0=ALU.add, op1=ALU.mult).then_inc(hid_ready, 1)
                    final = s + 1 == SEQS
                    if not final:
                        normal(n, s + 1)
                    if final:
                        rotate(n + SEQS, 0, "k0")
                    dve.wait_ge(ffn_full, n + s + 1 + 1)
                    dve.scalar_tensor_tensor(out=z[:, s * T:(s + 1) * T], in0=(SC if final else PJ)[0][:, :],
                                             scalar=vec[:, 2 * FBLK:2 * FBLK + 1], in1=z[:, s * T:(s + 1) * T],
                                             op0=ALU.add, op1=ALU.add).then_inc(z_ffn, 1)
                    if s == 0:
                        dve.wait_ge(z_ffn, n + s + 2)
                        shift_first(0, n + SEQS)
                        shift_rest(0, n + SEQS)
                        factors(L + 1)
                    elif not final:
                        split_weights(L + 1, PROJ[3 * s - 3:3 * s])
                rotate(n + SEQS, 0, "q0")
                norms(n + SEQS, 0, 0)
                rotate(n + SEQS, 0, "k1")
                rotate(n + SEQS, 0, "q1")
                norms(n + SEQS, 0, 1)

            dve.sem_inc(ffn_full, 1)
            factors(0)
            split_weights(0, PROJ)
            for w in ROT:
                rotate(0, 0, w)
                if ROT.index(w) % 2 == 1:
                    norms(0, 0, ROT.index(w) // 2)
            with dve.Fori(0, DEPTH) as L:
                sequences(dve, L, sequence)
                feed_forward(L)
            dve.wait_ge(z_ffn, DEPTH * SEQS + 1)
            dve.scalar_tensor_tensor(out=M.x[:, :], in0=z[:, :], scalar=0.5, in1=M.x[:, :],
                                     op0=ALU.mult, op1=ALU.add).then_inc(x_added, 1)


def full_attention_block(nc, M, W):
    GROUP = 4 * TILES
    UNITS = AH * TILES
    MIX, TURN, PV = 3, 4, 5
    with ExitStack() as ctx:
        sem = stage_semaphores(nc, ctx, "full")
        sb = lambda n, s, d=F32: ctx.enter_context(nc.sbuf_tensor(f"full_{n}", s, d))
        proj_full, part_ready, rest_ready, v_ready, q_stacked, k_stacked = (
            sem(n) for n in ("proj_full", "part_ready", "rest_ready", "v_ready", "q_stacked", "k_stacked"))
        stack_full, stack_act, stack_dve, prepared = (
            sem(n) for n in ("stack_full", "stack_act", "stack_dve", "prepared"))
        score_full, max_ready, exp_done, recip_ready, coef_ready, weighted, mixed = (
            sem(n) for n in ("score_full", "max_ready", "exp_done", "recip_ready", "coef_ready", "weighted", "mixed"))
        pt_full, pt_ready, out_full, out_ready, y_full, x_updated, cleared = (
            sem(n) for n in ("pt_full", "pt_ready", "out_full", "out_ready", "y_full", "x_updated", "cleared"))
        coefs = sb("coefs", [P, 2])
        part = sb("part", [P, 2, SPLITS, 3 * D], BF16)
        rest = sb("rest", [P, 2, 2, 3 * D])
        stack = sb("stack", [P, TILES, 3, AH, STACK], BF16)
        QK = sb("QK", [STACK, 3, AH, T], BF16)
        V = sb("V", [P, TILES, AH, 32])
        negmax = sb("negmax", [P, 4, 2])
        total = sb("total", [P, 4, 2])
        recip = sb("recip", [P, 4, 2])
        weight = sb("weight", [P, 4, 2])
        prob = sb("prob", [P, 4, 2, T])
        PT = sb("PT", [P, 2, TILES, P])
        outT = sb("outT", [P, 2, T])
        xcur = sb("xcur", [P, T])
        xcur_ready = sem("xcur_ready")
        passed, pool_passed = sem("passed"), sem("pool_passed")
        block = ctx.enter_context(nc.Block())
        B = M.bank
        QK_flat = QK[:, :, :, :].rearrange("r y h t -> r (y h t)")

        def rows(s, u):
            return s * UNITS + u

        @block.tensor
        def _(pe):
            pe.wait_ge(M.full_loaded, 16 * M.full_dmas)
            pe.wait_ge(cleared, 3)
            with pe.Fori(0, SEQS) as s:
                for i in range(TILES):
                    if i == 0:
                        pe.wait_ge(exp_done, rows(s, 2))
                        pe.wait_ge(xcur_ready, s + 1)
                    pe.matmul(B[i][:, :], xcur[:, i * P:(i + 1) * P], M.w4[:, :],
                              start=True, stop=True).then_inc(proj_full, 1)
                for c in range(3 * AH // 2):
                    if c == 0:
                        pe.wait_ge(q_stacked, s * TILES + TILES)
                        pe.wait_ge(k_stacked, s * TILES + TILES)
                        pe.wait_ge(pt_ready, rows(s, 2))
                        pe.wait_ge(out_ready, s * 4 + 1)
                        pe.wait_ge(x_updated, s + 1)
                    if c >= 4:
                        pe.wait_ge([stack_act, stack_dve][c % 2], s * 12 + (c // 2 - 1))
                    bank16 = B[4 + c % 4][0:STACK, :].bitcast(BF16)
                    y, hp = c // (AH // 2), c % (AH // 2)
                    for hh in range(2):
                        for i in range(TILES):
                            mm = pe.transpose(bank16[:, hh * T + i * P:hh * T + (i + 1) * P],
                                              stack[:, i, y, 2 * hp + hh, :], M.ident16[:, :])
                    mm.then_inc(stack_full, 1)
                pe.wait_ge(stack_act, s * 12 + 12)
                pe.wait_ge(stack_dve, s * 12 + 12)
                pe.wait_ge(v_ready, s * TILES + TILES)

                def project(g):
                    pe.wait_ge(out_ready, s * 4 + (g + 2))
                    pe.matmul(B[7][:, :], M.wo_full[:, g * D:(g + 1) * D], outT[:, g % 2, :],
                              start=(g == 0), stop=(g == 3)).then_inc(y_full, 1)

                for n in range(UNITS + PV):
                    if n < UNITS:
                        h, i = n // TILES, n % TILES
                        pe.wait_ge(exp_done, rows(s, n + 1))
                        for y in range(2):
                            mm = pe.matmul(B[2 * (n % 2) + y][:, :], QK[:, 0, h, i * P:(i + 1) * P],
                                           QK[:, 1 + y, h, :], start=True, stop=True)
                        mm.then_inc(score_full, 1)
                    if TURN <= n < UNITS + TURN:
                        u = n - TURN
                        pe.wait_ge(mixed, rows(s, u + 1))
                        pe.wait_ge(pt_ready, rows(s, u + 1))
                        for kb in range(TILES):
                            mm = pe.transpose(B[4 + u % 2][:, kb * P:(kb + 1) * P],
                                              prob[:, u % 4, 0, kb * P:(kb + 1) * P], M.ident[:, :])
                        mm.then_inc(pt_full, 1)
                    if n >= PV:
                        u = n - PV
                        h, i, j = u // TILES, u % TILES, u // TILES % 4
                        pe.wait_ge(pt_ready, rows(s, u + 1 + 2))
                        if u % GROUP == 0:
                            pe.wait_ge(out_ready, s * 4 + (u // GROUP + 1))
                        for kb in range(TILES):
                            mm = pe.matmul(B[6][32 * j:32 * j + 32, i * P:(i + 1) * P], V[:, kb, h, :],
                                           PT[:, u % 2, kb, :], start=(kb == 0), stop=(kb == TILES - 1))
                        mm.then_inc(out_full, 1)
                        if u % GROUP == 2 and u > GROUP:
                            project(u // GROUP - 1)
                project(3)

        @block.scalar
        def _(act):
            act.sem_inc(exp_done, 2)
            act.sem_inc(out_ready, 1)
            with act.Fori(0, SEQS) as s:
                for i in range(TILES):
                    act.wait_ge(proj_full, s * TILES + (i + 2))
                    b = i % 2
                    if i >= 2:
                        act.wait_ge(q_stacked, s * TILES + (i - 1))
                        act.wait_ge(k_stacked, s * TILES + (i - 1))
                    act.activation(V[:, i, :, 0:AD], B[i][:, 3 * D:4 * D].rearrange("p (h d) -> p h d", d=AD),
                                   ACT.Copy).then_inc(v_ready, 1)
                    act.activation(part[:, b, 0, :], B[i][:, 0:3 * D], ACT.Copy).then_inc(part_ready, 1)
                    for a in range(1, SPLITS):
                        act.wait_ge(rest_ready, s * (2 * TILES) + (2 * i + a))
                        act.activation(part[:, b, a, :], rest[:, b, a - 1, :], ACT.Copy).then_inc(part_ready, 1)
                for c in range(0, 3 * AH // 2, 2):
                    act.wait_ge(stack_full, s * 24 + (c + 2))
                    act.activation(QK_flat[:, c * 2 * T:(c + 1) * 2 * T], B[4 + c % 4][0:STACK, :].bitcast(BF16),
                                   ACT.Copy).then_inc(stack_act, 1)
                for n in range(UNITS + PV):
                    if n < UNITS:
                        act.wait_ge(max_ready, rows(s, n + 1))
                        act.wait_ge(pt_full, rows(s, n + 1))
                        for y in range(2):
                            last = act.activation(prob[:, n % 4, y, :], B[2 * (n % 2) + y][:, :], ACT.Exp,
                                                  bias=negmax[:, n % 4, y:y + 1], accum_out=total[:, n % 4, y:y + 1])
                        last.then_inc(exp_done, 1)
                    if TURN <= n < UNITS + TURN:
                        u = n - TURN
                        act.wait_ge(pt_full, rows(s, u + 1 + 4))
                        act.wait_ge(out_full, rows(s, u + 1))
                        act.activation(PT[:, u % 2, :, :], B[4 + u % 2][:, :].rearrange("p (k t) -> p k t", t=P),
                                       ACT.Copy).then_inc(pt_ready, 1)
                    if n >= PV and (n - PV) % GROUP == GROUP - 1:
                        g = (n - PV) // GROUP
                        act.wait_ge(out_full, rows(s, (g + 1) * GROUP + 2))
                        act.wait_ge(y_full, s * 4 + (g + 1))
                        act.activation(outT[:, g % 2, :], B[6][:, :], ACT.Copy).then_inc(out_ready, 1)

        @block.gpsimd
        def _(pool):
            pool.sem_inc(pt_ready, 2)
            pool.sem_inc(pt_full, 4)
            pool.sem_inc(out_full, 2)
            pool.sem_inc(y_full, 2)
            pool.memset(V[:, :, :, :], 0.0).then_inc(cleared, 1)
            with pool.Fori(0, SEQS) as s:
                for i in range(TILES):
                    for a in range(SPLITS):
                        pool.wait_ge(part_ready, s * (SPLITS * TILES) + (SPLITS * i + a + 1))
                        pool.sem_inc(pool_passed, 1)
                        last = pool.tensor_copy(
                            stack[:, i, 0, :, :].rearrange("p h (a b d) -> p h a b d", a=SPLITS, d=AD)[:, :, a, :, :],
                            part[:, i % 2, a, 0:D].rearrange("p (h o d) -> p h o d", o=1, d=AD)
                            .broadcast_to([P, AH, SPLITS, AD]))
                    last.then_inc(q_stacked, 1)
                for n in range(UNITS):
                    pool.wait_ge(coef_ready, rows(s, n + 1))
                    pool.tensor_tensor(prob[:, n % 4, 0, :], prob[:, n % 4, 0, :],
                                       weight[:, n % 4, 0:1].broadcast_to([P, T]), ALU.mult).then_inc(weighted, 1)

        @block.vector
        def _(dve):
            dve.sem_inc(x_updated, 1)
            dve.sem_inc(proj_full, 1)
            dve.sem_inc(stack_full, 1)
            dve.wait_ge(M.full_loaded, 16 * M.full_dmas)
            dve.tensor_scalar(coefs[:, 1:2], M.alpha[:, :], -1.0, 1.0, ALU.mult, ALU.add)
            dve.tensor_copy(coefs[:, 0:1], M.alpha[:, :]).then_inc(cleared, 1)
            dve.tensor_scalar(M.w4[:, 0:D], M.w4[:, 0:D], AD ** -0.5, None, ALU.mult).then_inc(cleared, 1)
            dve.wait_ge(cleared, 3)
            with dve.Fori(0, SEQS) as s:
                dve.wait_ge(proj_full, s * TILES + 1)
                dve.tensor_copy(xcur[:, :], M.xh[:, ds(s * T, T)]).then_inc(xcur_ready, 1)
                for i in range(TILES):
                    b = i % 2
                    dve.wait_ge(part_ready, s * (SPLITS * TILES) + (SPLITS * i + 1))
                    if i == 0:
                        dve.wait_ge(stack_full, s * 24 + 1)
                    dve.tensor_tensor(rest[:, b, 0, :], B[i][:, 0:3 * D], part[:, b, 0, :], ALU.subtract).then_inc(rest_ready, 1)
                    dve.wait_ge(part_ready, s * (SPLITS * TILES) + (SPLITS * i + 2))
                    dve.wait_ge(rest_ready, s * (2 * TILES) + (2 * i + 1))
                    dve.tensor_tensor(rest[:, b, 1, :], rest[:, b, 0, :], part[:, b, 1, :], ALU.subtract).then_inc(rest_ready, 1)
                    dve.wait_ge(part_ready, s * (SPLITS * TILES) + (SPLITS * i + 3))
                    for a in range(SPLITS):
                        last = dve.tensor_copy(
                            stack[:, i, 1:3, :, :].rearrange("p y h (b a d) -> p (y h) b a d", a=SPLITS, d=AD)[:, :, :, a, :],
                            part[:, b, a, D:3 * D].rearrange("p (h o d) -> p h o d", o=1, d=AD)
                            .broadcast_to([P, 2 * AH, SPLITS, AD]))
                    last.then_inc(k_stacked, 1)
                for c in range(1, 3 * AH // 2, 2):
                    dve.wait_ge(stack_full, s * 24 + (c + 2))
                    dve.tensor_copy(QK_flat[:, c * 2 * T:(c + 1) * 2 * T],
                                    B[4 + c % 4][0:STACK, :].bitcast(BF16)).then_inc(stack_dve, 1)
                for n in range(UNITS + MIX):
                    if n >= MIX:
                        u = n - MIX
                        dve.wait_ge(weighted, rows(s, u + 1))
                        dve.scalar_tensor_tensor(out=prob[:, u % 4, 0, :], in0=prob[:, u % 4, 1, :],
                                                 scalar=weight[:, u % 4, 1:2], in1=prob[:, u % 4, 0, :],
                                                 op0=ALU.mult, op1=ALU.add).then_inc(mixed, 1)
                    if n < UNITS:
                        dve.wait_ge(score_full, rows(s, n + 1))
                        dve.tensor_reduce(negmax[:, n % 4, :], M.psum[:, 2 * (n % 2):2 * (n % 2) + 2, :],
                                          AX_X, ALU.max, negate=True).then_inc(max_ready, 1)
                    if 1 <= n <= UNITS:
                        u = n - 1
                        dve.wait_ge(exp_done, rows(s, u + 1 + 2))
                        dve.reciprocal(recip[:, u % 4, :], total[:, u % 4, :]).then_inc(recip_ready, 1)
                        dve.wait_ge(recip_ready, rows(s, u + 1))
                        dve.tensor_tensor(weight[:, u % 4, :], recip[:, u % 4, :], coefs[:, :], ALU.mult).then_inc(coef_ready, 1)
                dve.wait_ge(y_full, s * 4 + 6)
                dve.tensor_tensor(M.x[:, ds(s * T, T)], M.x[:, ds(s * T, T)], B[7][:, :], ALU.add).then_inc(x_updated, 1)


def program(nc, A, out):
    M = Shared()
    with ExitStack() as ctx:
        sb = lambda n, s, d=F32: ctx.enter_context(nc.sbuf_tensor(n, s, d))
        sem = lambda n: ctx.enter_context(nc.semaphore(n))
        M.psum = ctx.enter_context(nc.psum_tensor("psum", [P, 8, 512], F32))
        M.bank = [M.psum[:, b, :] for b in range(8)]
        M.x = sb("x", [P, NTOK])
        M.xh = sb("xh", [P, NTOK])
        M.z = M.xh
        M.ident = sb("ident", [P, P])
        M.ident16 = sb("ident16", [P, P], BF16)
        M.mean_w = sb("mean_w", [P, P])
        M.tables = sb("tables", [P, 4, TILES, DH])
        mask32 = sb("mask32", [P, 2, 2 * KEYS])
        M.mask = sb("mask", [P, 2, 2 * KEYS], BF16)
        M.w4 = sb("w4", [P, 4 * D])
        M.wo_full = sb("wo_full", [P, 4 * D])
        M.alpha = sb("alpha", [P, 1])
        x_loaded, const_loaded, consts = sem("x_loaded"), sem("const_loaded"), sem("consts")
        M.moe_loaded, M.lin_loaded, M.full_loaded, stored = (
            sem("moe_loaded"), sem("lin_loaded"), sem("full_loaded"), sem("stored"))

        with ExitStack() as moe:
            sbm = lambda n, s, d=F32: moe.enter_context(nc.sbuf_tensor(n, s, d))
            M.wg = sbm("wg", [P, EXPERTS])
            M.bg = sbm("bg", [P, EXPERTS])
            M.b1 = sbm("moe_b1", [P, EXPERTS * HBLK])
            M.b2 = sbm("moe_b2", [EXPERTS, D])
            M.wq, M.wk, M.wv, M.wo_lin = (sbm(n, [P, LIN_HEADS // 2 * D]) for n in ("lin_wq", "lin_wk", "lin_wv", "lin_wo"))
            moe_loads = [(M.wg, "wg"), (M.b1, "moe_b1"), (M.b2, "moe_b2")]
            M.moe_dmas = len(moe_loads) + 1
            M.lin_dmas = 4
            M.full_dmas = 3
            with nc.Block() as block:
                @block.sync
                def _(sp):
                    for s in range(SEQS):
                        sp.dma_start(M.x[:, s * T:(s + 1) * T], A["xT"][:, s * T:(s + 1) * T]).then_inc(x_loaded, 16)
                    sp.dma_start(M.ident[:, :], A["ident"]).then_inc(const_loaded, 16)
                    sp.dma_start(mask32[:, :, :], A["mask"].rearrange("p (a k) -> p a k", a=2)).then_inc(const_loaded, 16)
                    sp.dma_start(M.tables[:, :, :, :], A["tables"].rearrange("p (a i d) -> p a i d", a=4, d=DH)).then_inc(const_loaded, 16)
                    for t, n in moe_loads:
                        sp.dma_start(t[:, :], A[n]).then_inc(M.moe_loaded, 16)
                    sp.dma_start(M.bg[:, :], A["bg"].broadcast_to([P, EXPERTS])).then_inc(M.moe_loaded, 16)
                    for t, n in ((M.wq, "lin_wq"), (M.wk, "lin_wk"), (M.wv, "lin_wv"), (M.wo_lin, "lin_wo")):
                        sp.dma_start(t[:, :], A[n]).then_inc(M.lin_loaded, 16)
                    sp.dma_start(M.w4[:, :], A["w4"]).then_inc(M.full_loaded, 16)
                    sp.dma_start(M.wo_full[:, :], A["wo_full"]).then_inc(M.full_loaded, 16)
                    sp.dma_start(M.alpha[:, :], A["alpha"].broadcast_to([P, 1])).then_inc(M.full_loaded, 16)
                    sp.wait_ge(x_loaded, 16 * SEQS)

                @block.vector
                def _(dve):
                    dve.memset(M.mean_w[:, :], 1.0 / D).then_inc(consts, 1)
                    dve.wait_ge(const_loaded, 48)
                    dve.tensor_copy(M.ident16[:, :], M.ident[:, :]).then_inc(consts, 1)
                    dve.tensor_copy(M.mask[:, :, :], mask32[:, :, :]).then_inc(consts, 1)

            layernorm_block(nc, M, M.x, M.xh, "ln0")
            expert_block(nc, M, A, "moe0")
            layernorm_block(nc, M, M.x, M.xh, "ln1")
            linear_attention_block(nc, M)
            layernorm_block(nc, M, M.x, M.xh, "ln2")
            expert_block(nc, M, A, "moe1")
        layernorm_block(nc, M, M.x, M.xh, "ln3")
        local_transformer_block(nc, M, A, "loc0")
        layernorm_block(nc, M, M.x, M.xh, "ln4")
        full_attention_block(nc, M, A)
        layernorm_block(nc, M, M.x, M.xh, "ln5")
        local_transformer_block(nc, M, A, "loc1")
        with nc.Block() as block:
            @block.sync
            def _(sp):
                sp.dma_start(out, M.x[:, :]).then_inc(stored, 16)
                for loaded, n in ((M.moe_loaded, M.moe_dmas), (M.lin_loaded, M.lin_dmas), (M.full_loaded, M.full_dmas)):
                    sp.wait_ge(loaded, 16 * n)
                sp.wait_ge(stored, 16)


def rotary_constants():
    f = np.float32
    half = np.arange(0, DH, 2).astype(f)
    inv_freq = f(1.0) / np.power(f(10000.0), half / f(DH)).astype(f)
    t = np.arange(T).astype(f)
    freqs = (t[:, None] * inv_freq[None, :]).astype(f)
    base = (half + f(0.4 * DH)) / f(1.4 * DH)
    power = (t - f(T // 2)) / f(WINDOW // 2)
    scale = np.power(base[None, :], power[:, None]).astype(f)
    cos, sin = np.cos(freqs.astype(np.float64)), np.sin(freqs.astype(np.float64))
    sc = scale.astype(np.float64)
    twice = lambda a, b: np.concatenate([a, b], -1)
    tabs = [twice(cos * sc, cos * sc) * QK_SCALE, twice(-sin * sc, sin * sc) * QK_SCALE,
            twice(cos / sc, cos / sc), twice(-sin / sc, sin / sc)]
    tab = np.stack(tabs).astype(f)
    return np.ascontiguousarray(tab.reshape(4, TILES, P, DH).transpose(2, 0, 1, 3).reshape(P, -1))


def mask_constant():
    q = np.arange(P)[:, None]
    c = np.arange(KEYS)[None, :]
    seen = (q <= c) & (c <= q + WINDOW)
    later = np.where(seen, 0.0, MASKED)
    firsts = np.where(seen & (c >= WINDOW), 0.0, MASKED)
    return np.concatenate([firsts, firsts, later, later], 1).astype(np.float32)


def layout(I):
    c = np.ascontiguousarray
    I = {k: np.asarray(v) for k, v in I.items()}
    pairs = lambda w: c(w.reshape(LIN_HEADS // 2, P, D).transpose(1, 0, 2).reshape(P, -1))
    L1 = "L1_ffn_"
    b1, vecs = I[L1 + "b1"], np.zeros((DEPTH, P, 2 * FBLK + 3), np.float32)
    w2 = np.zeros((DEPTH, P, FBLK, D), np.float32)
    for k in range(FBLK):
        n = blk(k)
        vecs[:, :n, k] = b1[:, k * P:k * P + n]
        vecs[:, :n, FBLK + k] = b1[:, FF + k * P:FF + k * P + n]
        w2[:, :n, k] = I[L1 + "W2"][:, k * P:k * P + n]
    for j, n in enumerate(("b2", "ln_g", "ln_b")):
        vecs[:, :, 2 * FBLK + j] = I[L1 + n]
    qs, ks = I[L1 + "q_scale"], I[L1 + "k_scale"]
    swap = lambda a: np.concatenate([a[:, DH // 2:], a[:, :DH // 2]], 1)
    wo_full = np.zeros((4, 4, 32, D), np.float32)
    wo_full[:, :, :AD] = I["L1_attn_W_O"].T.reshape(4, 4, AD, D)
    return {
        "xT": c(I["L0_attn_x"].reshape(NTOK, D).T),
        "ident": np.eye(P, dtype=np.float32), "mask": mask_constant(), "tables": rotary_constants(),
        "wg": I["L0_ffn_Wg"], "bg": I["L0_ffn_bg"].reshape(1, EXPERTS),
        "moe_w1": c(I["L0_ffn_W1"].transpose(1, 0, 2).reshape(D, -1)),
        "moe_w2": c(I["L0_ffn_W2"].reshape(EXPERTS, HBLK, P, D).transpose(2, 0, 1, 3).reshape(P, -1)),
        "moe_b1": c(I["L0_ffn_b1"].reshape(EXPERTS * HBLK, P).T), "moe_b2": I["L0_ffn_b2"],
        "lin_wq": pairs(I["L0_attn_W_q"]), "lin_wk": pairs(I["L0_attn_W_k"]), "lin_wv": pairs(I["L0_attn_W_v"]),
        "lin_wo": pairs(c(I["L0_attn_W_o"].T)),
        "w4": c(np.concatenate([I["L1_attn_" + n].T for n in ("W_Q", "W_K", "W_K_prime", "W_V")], 1)),
        "wo_full": c(wo_full.transpose(1, 2, 0, 3).reshape(P, -1)),
        "alpha": I["L1_attn_alpha"].reshape(1, 1),
        "wqkv": np.concatenate([I[L1 + "Wqkv"], np.zeros((1, D, 3 * INNER), np.float32)]),
               "w1": I[L1 + "W1"], "w2": c(w2.reshape(DEPTH, P, -1)), "vec": vecs,
        "wo": c(I[L1 + "Wo"].reshape(DEPTH, PAIRS, P, D).transpose(0, 2, 1, 3).reshape(DEPTH, P, -1)),
        "scales": np.concatenate([np.concatenate([qs, swap(qs), ks, swap(ks)], 1), np.zeros((1, 4 * DH), np.float32)]),
    }


def kernel(**I):
    import concourse.bacc as bacc
    from concourse.bass_utils import run_bass_kernel_spmd

    c = np.ascontiguousarray
    arrays = layout(I)
    nc = bacc.Bacc("TRN2", target_bir_lowering=False, num_devices=1)
    A = {n: nc.dram_tensor("in_" + n, a.shape, mybir.dt.from_np(a.dtype), kind="ExternalInput").ap() for n, a in arrays.items()}
    out = nc.dram_tensor("out_xT", (D, NTOK), F32, kind="ExternalOutput").ap()
    program(nc, A, out)
    r = run_bass_kernel_spmd(nc, [{"in_" + n: c(a) for n, a in arrays.items()}], core_ids=[0])
    return c(r.results[0]["out_xT"].T).reshape(SEQS, T, D)
```
